# Optimizing a Trainium2 kernel written in Bass

```python
import numpy as np
import jax
import jax.numpy as jnp

def _softmax(x, axis=-1):
    return jax.nn.softmax(x, axis=axis)

def _gelu(x):
    return jax.nn.gelu(x, approximate=True)

def _silu(x):
    return jax.nn.silu(x)

def _sigmoid(x):
    return jax.nn.sigmoid(x)

def _layernorm(x, axis=-1, eps=1e-05):
    m = jnp.mean(x, axis=axis, keepdims=True)
    v = jnp.var(x, axis=axis, keepdims=True)
    return (x - m) / jnp.sqrt(v + eps)

def _scatter_add(tgt, idx, src, axis=0):
    return tgt.at[idx].add(src)

def _segment_sum(src, seg, n):
    return jax.ops.segment_sum(src, seg, n)
kernel_name = 'mk_xattn_ffn_d1_seqx_r4_7b0150'

def setup_inputs(seed: int=0):
    np.random.seed(seed)
    _w = jnp.asarray

    def _rec_inputs():
        import jax
        import jax.numpy as jnp
        _rk = jax.random.key(seed)
        x = 7.22e-05 + 1 * jax.random.normal(jax.random.fold_in(_rk, 1), (8, 256, 256), jnp.float32)
        _lenS = 256 - jax.random.randint(jax.random.fold_in(_rk, 7), (8,), 0, max(1, 256 // 4) + 1, jnp.int32)
        _lenS2 = 256 - jax.random.randint(jax.random.fold_in(_rk, 8), (8,), 0, max(1, 256 // 4) + 1, jnp.int32)
        _ctx_1024P = jax.random.normal(jax.random.fold_in(_rk, 11), (8, 16, 256), jnp.float32)
        _ctx_1024c = jax.random.dirichlet(jax.random.fold_in(_rk, 511), 0.3 * jnp.ones((16,), jnp.float32), (8, 256))
        _ctx_1024t = jnp.einsum('bsk,bkd->bsd', _ctx_1024c, _ctx_1024P)
        _ctx_1024t = _ctx_1024t * jax.lax.rsqrt(jnp.mean(jnp.square(_ctx_1024t)) + 1e-12) * 0.953939
        ctx_1024 = 4.13588e-05 + 0.999923 * (_ctx_1024t + 0.3 * jax.random.normal(jax.random.fold_in(_rk, 611), (8, 256, 256), jnp.float32))
        _validS = jnp.arange(256)[None, :] < _lenS[:, None]
        _validS2 = jnp.arange(256)[None, :] < _lenS2[:, None]
        _causal = jnp.tril(jnp.ones((256, 256), dtype=bool))
        mask_BxS2_bf1 = jnp.ones((8, 256), dtype=bool)
        mask_BxSxS2_bf1 = jnp.ones((8, 256, 256), dtype=bool)
        return (x, ctx_1024, mask_BxS2_bf1, mask_BxSxS2_bf1)
    x, ctx_1024, mask_BxS2_bf1, mask_BxSxS2_bf1 = _rec_inputs()

    def _L0_xattn_setup():
        import jax, jax.numpy as jnp
        import numpy as np
        N, L, E, H = (4, 512, 256, 16)
        D = E // H
        key = jax.random.key(seed)
        ks = jax.random.split(key, 8)
        s = 1.0 / np.sqrt(E)
        return {'Q': jax.random.normal(ks[0], (N, L, E), jnp.float32), 'K': jax.random.normal(ks[1], (N, L, E), jnp.float32), 'V': jax.random.normal(ks[2], (N, L, E), jnp.float32), 'Wq': jax.random.normal(ks[3], (E, E), jnp.float32) * s, 'Wk': jax.random.normal(ks[4], (E, E), jnp.float32) * s, 'Wv': jax.random.normal(ks[5], (E, E), jnp.float32) * s, 'Wo': jax.random.normal(ks[6], (E, E), jnp.float32) * s, 'bo': jax.random.normal(ks[7], (E,), jnp.float32) * s, 'padding_mask': jnp.ones((N, L), dtype=bool), 'attention_mask': jnp.ones((N, L, L), dtype=bool)}
    _L0_xattn_all = _L0_xattn_setup()
    _L0_xattn_in = {k: v for k, v in _L0_xattn_all.items() if k in ('Wq', 'Wk', 'Wv', 'Wo', 'bo')}
    del _L0_xattn_all

    def _L0_ffn_setup():
        import jax, jax.numpy as jnp
        import numpy as np
        D_MODEL = 256
        N_EXPERTS = 8
        TOP_K = 2
        FFN_HIDDEN = 4 * D_MODEL
        key = jax.random.key(seed)
        ks = jax.random.split(key, 6)

        def xavier(k, shape):
            fan_in, fan_out = (shape[-2], shape[-1])
            lim = jnp.sqrt(6.0 / (fan_in + fan_out))
            return jax.random.uniform(k, shape, jnp.float32, -lim, lim)
        x = jax.random.normal(ks[0], (4, 512, D_MODEL), jnp.float32)
        w_gate = xavier(ks[1], (N_EXPERTS, D_MODEL))
        W1 = xavier(ks[2], (N_EXPERTS, D_MODEL, FFN_HIDDEN))
        b1 = jnp.zeros((N_EXPERTS, FFN_HIDDEN), jnp.float32)
        W2 = xavier(ks[3], (N_EXPERTS, FFN_HIDDEN, D_MODEL))
        b2 = jnp.zeros((N_EXPERTS, D_MODEL), jnp.float32)
        return {'x': x, 'w_gate': w_gate, 'W1': W1, 'b1': b1, 'W2': W2, 'b2': b2}
    _L0_ffn_all = _L0_ffn_setup()
    _L0_ffn_in = {k: v for k, v in _L0_ffn_all.items() if k in ('w_gate', 'W1', 'b1', 'W2', 'b2')}
    del _L0_ffn_all
    return {'x': x, 'ctx_1024': ctx_1024, 'mask_BxS2_bf1': mask_BxS2_bf1, 'mask_BxSxS2_bf1': mask_BxSxS2_bf1, 'L0_xattn_Wq': _L0_xattn_in['Wq'], 'L0_xattn_Wk': _L0_xattn_in['Wk'], 'L0_xattn_Wv': _L0_xattn_in['Wv'], 'L0_xattn_Wo': _L0_xattn_in['Wo'], 'L0_xattn_bo': _L0_xattn_in['bo'], 'L0_ffn_w_gate': _L0_ffn_in['w_gate'], 'L0_ffn_W1': _L0_ffn_in['W1'], 'L0_ffn_b1': _L0_ffn_in['b1'], 'L0_ffn_W2': _L0_ffn_in['W2'], 'L0_ffn_b2': _L0_ffn_in['b2']}

def reference(x, ctx_1024, mask_BxS2_bf1, mask_BxSxS2_bf1, L0_xattn_Wq, L0_xattn_Wk, L0_xattn_Wv, L0_xattn_Wo, L0_xattn_bo, L0_ffn_w_gate, L0_ffn_W1, L0_ffn_b1, L0_ffn_W2, L0_ffn_b2):
    import jax
    import jax.numpy as jnp

    def _L0_xattn_ref(Q, K, V, Wq, Wk, Wv, Wo, bo, padding_mask, attention_mask):
        import jax, jax.numpy as jnp
        import numpy as np
        N, L, E, H = (4, 512, 256, 16)
        D = E // H
        n, lq, e = Q.shape
        q = jnp.einsum('nle,fe->nlf', Q, Wq).reshape(n, lq, H, D).transpose(0, 2, 1, 3)
        k = jnp.einsum('nle,fe->nlf', K, Wk).reshape(n, -1, H, D).transpose(0, 2, 1, 3)
        v = jnp.einsum('nle,fe->nlf', V, Wv).reshape(n, -1, H, D).transpose(0, 2, 1, 3)
        attn = jnp.einsum('nhqd,nhkd->nhqk', q, k) / jnp.sqrt(jnp.asarray(D, q.dtype))
        neg_inf = jnp.asarray(-jnp.inf, attn.dtype)
        attn = jnp.where(padding_mask[:, None, :, None], attn, neg_inf)
        attn = jnp.where(attention_mask[:, None], attn, neg_inf)
        p = jax.nn.softmax(attn, axis=-1)
        out = jnp.einsum('nhqk,nhkd->nhqd', p, v)
        out = out.transpose(0, 2, 1, 3).reshape(n, lq, e)
        return jnp.einsum('nle,fe->nlf', out, Wo) + bo

    def _L0_ffn_ref(x, w_gate, W1, b1, W2, b2):
        import jax, jax.numpy as jnp
        import numpy as np
        D_MODEL = 256
        N_EXPERTS = 8
        TOP_K = 2
        FFN_HIDDEN = 4 * D_MODEL
        B, S, D = x.shape
        flat_x = x.reshape(-1, D)
        gate = jax.nn.softmax(flat_x @ w_gate.T, axis=-1)
        topk_scores, topk_idx = jax.lax.top_k(gate, TOP_K)
        cw = (jax.nn.one_hot(topk_idx, N_EXPERTS, dtype=flat_x.dtype) * topk_scores[..., None]).sum(axis=1)
        h = jax.nn.gelu(jnp.einsum('td,edh->teh', flat_x, W1) + b1, approximate=False)
        y = jnp.einsum('teh,ehd->ted', h, W2) + b2
        out = jnp.einsum('ted,te->td', y, cw)
        return out.reshape(B, S, D)
    x = x + _L0_xattn_ref(_layernorm(x, axis=-1), ctx_1024, ctx_1024, L0_xattn_Wq, L0_xattn_Wk, L0_xattn_Wv, L0_xattn_Wo, L0_xattn_bo, mask_BxS2_bf1, mask_BxSxS2_bf1)
    x = x + _L0_ffn_ref(_layernorm(x, axis=-1), L0_ffn_w_gate, L0_ffn_W1, L0_ffn_b1, L0_ffn_W2, L0_ffn_b2)
    return x

_drawn_inputs = setup_inputs


def setup_inputs(seed=0):
    import zlib

    import numpy as np

    out = dict(_drawn_inputs(seed))
    spreads = {'L0_ffn_b1': (0.0, 0.1), 'L0_ffn_b2': (0.0, 0.1)}
    factors = {}
    for name, (base, spread) in spreads.items():
        noise = np.random.default_rng([zlib.crc32(name.encode()), seed]).standard_normal(out[name].shape)
        drawn = base * np.exp(spread * noise) if base else spread * noise
        out[name] = jnp.asarray(drawn.astype(out[name].dtype))
    for name, factor in factors.items():
        out[name] = (out[name] * factor).astype(out[name].dtype)
    return out
```

```python
from contextlib import ExitStack

import numpy as np
import concourse.bass as bass
from concourse import mybir

F32 = mybir.dt.float32
F32R = mybir.dt.float32r
BF16 = mybir.dt.bfloat16
U8 = mybir.dt.uint8
ALU = mybir.AluOpType
ACT = mybir.ActivationFunctionType
AX = mybir.AxisListType

P = 128
STRIP = 32
LN_EPS = 1e-5
BIG = 2.0 ** 100


class Step:

    def __init__(self, ctx, nc, name, by=1):
        self.sem, self.by, self.count, self.waited = ctx.enter_context(nc.semaphore(name)), by, 0, {}

    def did(self, instruction):
        instruction.then_inc(self.sem, self.by)
        self.count += self.by

    def done(self):
        return self.count


def need(engine, step, count=None):
    count = step.count if count is None else count
    if count > step.waited.get(engine, 0):
        engine.wait_ge(step.sem, count)
        step.waited[engine] = count


def build(nc, x, ctx_in, pad, mask, Wq, Wk, Wv, Wo, bo, w_gate, W1, b1, W2, b2, out):
    pe, dve, act, pool, sp = nc.tensor, nc.vector, nc.scalar, nc.gpsimd, nc.sync
    NB, L, E = x.shape
    NE, _, F = W1.shape
    D = 16
    H = E // D
    TT = L // P
    KC = E // P
    NT = NB * TT
    HPT = P // STRIP
    MQ = H // HPT
    SCALE = 1.0 / float(np.sqrt(D))
    assert TT == 2 and KC == 2 and H == 16

    x_d = x.rearrange("n (t p) e -> n p t e", p=P)
    c_d = ctx_in.rearrange("n (t p) e -> n p t e", p=P)
    m_d = mask.rearrange("n (t p) k -> n p t k", p=P)
    out_d = out.rearrange("n (t p) e -> p (n t) e", p=P)

    top = ExitStack()
    with top:
        def step(name, by=1):
            return Step(top, nc, name, by)

        def sb(ctx, name, shape, dt=F32):
            return ctx.enter_context(nc.sbuf_tensor(name, shape, dt))

        ident = sb(top, "ident", [P, P])
        x2 = sb(top, "x2", [P, NT, E])
        XTh = sb(top, "XTh", [P, KC, NT * P], F32R)
        XTl = sb(top, "XTl", [P, KC, NT * P], F32R)
        logits = sb(top, "logits", [P, NT, NE])
        cw = sb(top, "cw", [P, NT, NE])
        b1T = sb(top, "b1T", [P, NE * F // P])
        b2r = sb(top, "b2r", [2, NE, E], F32R)
        ones2 = sb(top, "ones2", [2, P], F32R)

        A = ExitStack()
        bank = [A.enter_context(nc.psum_tensor(f"bank{i}", [P, 512], F32)) for i in range(8)]
        s1_bank, s2_bank, pv_bank, misc_bank = bank[0:2], bank[2:4], bank[4:6], bank[6:8]

        WqT = [sb(A, f"WqT{i}", [P, KC, MQ * P], F32R) for i in range(2)]
        WkT = [sb(A, f"WkT{i}", [P, KC, MQ * P], F32R) for i in range(2)]
        WvT = [sb(A, f"WvT{i}", [P, KC, E], F32R) for i in range(2)]
        WoT = [sb(A, f"WoT{i}", [P, KC, E], F32R) for i in range(2)]
        WgT = [sb(A, f"WgT{i}", [P, KC, NE], F32R) for i in range(2)]
        bo_b = sb(A, "bo_b", [P, E])
        mask16 = sb(A, "mask16", [P, D])
        neglo = sb(A, "neglo", [P, 1])
        sel = sb(A, "sel", [P, H, P], F32R)
        xin = [sb(A, f"xin{i}", [P, TT, E]) for i in range(3)]
        cin = [sb(A, f"cin{i}", [P, TT, E]) for i in range(2)]
        padB = sb(A, "padB", [P, NT])
        identb = sb(A, "identb", [P, P], BF16)
        min_ = [sb(A, f"min{i}", [P, TT, L], U8) for i in range(2)]
        Bq = [sb(A, f"Bq{i}", [P, TT, L], BF16) for i in range(3)]
        Bk = [sb(A, f"Bk{i}", [P, TT, L], BF16) for i in range(3)]
        free_ = sb(A, "free_", [P, TT])
        nanb = sb(A, "nanb", [P, TT])
        xb = [sb(A, f"xb{i}", [P, TT, E]) for i in range(4)]
        xn = sb(A, "xn", [P, TT, E])
        xT = [sb(A, f"xT{i}", [P, KC, L], F32R) for i in range(2)]
        cT = [sb(A, f"cT{i}", [P, KC, L], F32R) for i in range(2)]
        Qh = sb(A, "Qh", [P, 2 * L], F32R)
        Qm = [sb(A, f"Qm{i}", [P, MQ, L], F32R) for i in range(3)]
        K1 = [sb(A, f"K1{i}", [P, MQ, L], F32R) for i in range(3)]
        K2 = [sb(A, f"K2{i}", [P, MQ, L], F32R) for i in range(3)]
        V = [sb(A, f"V{i}", [P, TT, H, STRIP]) for i in range(3)]
        st6 = sb(A, "st6", [P, TT, 6])
        mv = sb(A, "mv", [P, TT, 2])
        ve = sb(A, "ve", [P, TT])
        rstd = sb(A, "rstd", [P, TT])
        st6b = sb(A, "st6b", [P, TT, 6])
        mvb = sb(A, "mvb", [P, TT, 2])
        veb = sb(A, "veb", [P, TT])
        rstdb = sb(A, "rstdb", [P, TT])
        half = sb(A, "half", [P, TT])
        nmax = [sb(A, f"nmax{i}", [P, H, TT]) for i in range(2)]
        mT = [sb(A, f"mT{i}", [P, L], F32R) for i in range(2)]

        first = ExitStack()
        Wst = sb(first, "Wst", [P, 4, TT, E])
        wg_in = sb(first, "wg_in", [NE, E])
        b1_in = sb(first, "b1_in", [NE * F // P, P])
        b2_in = sb(first, "b2_in", [2, NE, E])
        b2h = sb(first, "b2h", [2, NE, E], F32R)
        pad_in = sb(first, "pad_in", [NT, P], U8)
        pad_f = sb(first, "pad_f", [NT, P])

        ld_w = step("ld_w", 16)
        ld_x = [step(f"ld_x{i}", 16) for i in range(3)]
        ld_m = [step(f"ld_m{i}", 16) for i in range(2)]
        ld_c = [step(f"ld_c{i}", 16) for i in range(2)]
        st_out = step("st_out", 16)
        consts = step("consts")
        c_dve = step("c_dve")
        pe_misc = step("pe_misc")
        act_misc = step("act_misc")
        dve_misc = step("dve_misc")
        pe_s1 = step("pe_s1")
        dve_max = step("dve_max")
        pe_s2 = step("pe_s2")
        act_exp = step("act_exp")
        pe_pv = step("pe_pv")
        dve_ot = step("dve_ot")
        dve_ln = step("dve_ln")
        pool_ln = step("pool_ln")
        pool_xb = step("pool_xb")
        pool_v = step("pool_v")

        for i, w in enumerate((Wq, Wk, Wv, Wo)):
            ld_w.did(sp.dma_start(Wst[:, i], w.rearrange("(t p) e -> p t e", p=P)))
        ld_w.did(act.dma_start(pad_in[:], pad.rearrange("n (t p) -> (n t) p", p=P)))
        ld_w.did(act.dma_start(wg_in[:], w_gate))
        ld_w.did(act.dma_start(b1_in[:], b1.rearrange("e (m p) -> (e m) p", p=P)))
        for r in range(2):
            ld_w.did(act.dma_start(b2_in[r:r + 1], b2.rearrange("(o e) d -> o e d", o=1)))
        ld_w.did(act.dma_start(bo_b[:], bo.rearrange("(o e) -> o e", o=1).to_broadcast([P, E])))

        def load(n):
            need(sp, dve_ln)
            need(sp, pool_xb)
            need(sp, pe_misc)
            need(sp, dve_misc)
            ld_m[n % 2].did(sp.dma_start(min_[n % 2][:], m_d[n]))
            ld_x[n % 3].did(sp.dma_start(xin[n % 3][:], x_d[n]))
            ld_c[n % 2].did(sp.dma_start(cin[n % 2][:], c_d[n]))

        load(0)
        load(1)

        consts.did(pool.memset(ident[:], 0.0))
        consts.did(pool.memset(half[:], -0.5))
        need(pool, consts)
        consts.did(pool.affine_select(out=ident[:], in_=ident[:], compare_op=ALU.not_equal, fill=1.0, base=0,
                                      pattern=[[-1, P]], channel_multiplier=1))
        for i in range(3):
            pool_v.did(pool.memset(V[i][:, :, :, D:], 0.0))
        need(pool, pool_v)
        for i in range(3):
            pool_v.did(pool.memset(V[i][:, :, :, D:D + 1], 1.0))
        need(dve, consts)
        c_dve.did(dve.tensor_reduce(mask16[:], ident[:].rearrange("p (a h) -> p h a", h=D), AX.X, ALU.add))
        c_dve.did(dve.tensor_reduce(neglo[:], ident[:].rearrange("p (s h) -> p s h", h=STRIP)[:, :, D:], AX.XY,
                                    ALU.add, negate=True))
        c_dve.did(dve.memset(ones2[:].bitcast(F32), 1.0))
        need(dve, c_dve)
        c_dve.did(dve.tensor_copy(sel[:], mask16[:].rearrange("p (h o) -> p h o", o=1).to_broadcast([P, H, P])))
        need(dve, ld_w)
        c_dve.did(dve.tensor_copy(b2h[:], b2_in[:]))
        need(dve, c_dve)
        c_dve.did(dve.tensor_scalar(b2h[:], b2h[:].bitcast(F32), ident[0:2, 1:2], None, ALU.mult))
        c_dve.did(dve.tensor_copy(identb[:], ident[:]))
        c_dve.did(dve.tensor_copy(pad_f[:], pad_in[:]))
        need(dve, c_dve)
        c_dve.did(dve.tensor_tensor(b2r[:], b2_in[:], b2h[:].bitcast(F32), ALU.subtract))

        turn = [0]

        def misc():
            turn[0] += 1
            need(pe, act_misc)
            need(pe, dve_misc)
            return misc_bank[turn[0] % 2]

        def parts(src, hi, lo):
            need(act, pe_misc)
            act_misc.did(act.activation(hi, src, ACT.Copy))
            need(dve, act_misc)
            dve_misc.did(dve.tensor_tensor(lo, src, hi.bitcast(F32), ALU.subtract))

        need(pe, ld_w)
        need(pe, consts)
        for i in range(4):
            b = misc()
            for kc in range(KC):
                for fc in range(TT):
                    t = pe.transpose(b[:, kc * E + fc * P:kc * E + fc * P + P], Wst[:, i, fc, kc * P:kc * P + P],
                                     ident[:])
            pe_misc.did(t)
            if i < 2:
                hi, lo = (WqT, WkT)[i]
                for kc in range(KC):
                    src = b[:, kc * E:(kc + 1) * E].rearrange("p (h d) -> p h d", d=D)
                    for c in range(2):
                        def strip(w):
                            return w[:, kc, :].rearrange("p (h c d) -> p h c d", c=2, d=D)[:, :, c, :]
                        need(act, dve_misc)
                        parts(src, strip(hi), strip(lo))
            else:
                hi, lo = (WvT, WoT)[i - 2]
                parts(b[:].rearrange("p (k e) -> p k e", k=KC), hi[:], lo[:])
        b = misc()
        for kc in range(KC):
            pe.transpose(b[:, kc * NE:(kc + 1) * NE], wg_in[:, kc * P:(kc + 1) * P], ident[0:NE, 0:NE])
        nb1 = NE * F // P
        need(pe, c_dve)
        pe.transpose(b[:, 256:256 + NT], pad_f[:], ident[0:NT, 0:NT])
        pe_misc.did(pe.transpose(b[:, 64:64 + nb1], b1_in[:], ident[0:nb1, 0:nb1]))
        parts(b[:, 0:KC * NE].rearrange("p (k e) -> p k e", k=KC), WgT[0][:], WgT[1][:])
        dve_misc.did(dve.tensor_copy(b1T[:], b[:, 64:64 + nb1]))
        dve_misc.did(dve.tensor_scalar(padB[:], b[:, 256:256 + NT], BIG, None, ALU.mult))

        first.close()
        mrep = sb(A, "mrep", [P, TT, HPT, 2, H])
        prob = [sb(A, f"prob{i}", [P, TT, L]) for i in range(3)]
        OT = [sb(A, f"OT{i}", [P, L]) for i in range(4)]
        rden = sb(A, "rden", [P, H])
        ao = sb(A, "ao", [P, TT, E])
        aT = [sb(A, f"aT{i}", [P, KC, L], F32R) for i in range(2)]
        x2n = sb(A, "x2n", [P, TT, E])

        def pre_norm(n):
            xi = xin[n % 3]
            need(dve, ld_x[n % 3])
            for t in range(TT):
                dve_ln.did(dve.bn_stats(st6[:, t], xi[:, t]))
            need(dve, dve_ln)
            need(dve, pool_ln)
            for t in range(TT):
                dve_ln.did(dve.bn_aggr(mv[:, t], st6[:, t]))
            need(pool, dve_ln)
            pool_ln.did(pool.tensor_scalar(ve[:], mv[:, :, 1], LN_EPS, None, ALU.add))
            need(pool, pool_ln)
            pool_ln.did(pool.tensor_tensor(rstd[:], ve[:], half[:], ALU.pow))
            need(pool, ld_w)
            need(pool, ld_x[n % 3])
            need(pool, pool_xb)
            need(pool, dve_misc)
            for t in range(TT):
                pool_xb.did(pool.tensor_tensor(xb[n % 4][:, t], xi[:, t], bo_b[:], ALU.add))

        def pre_mask(n):
            need(dve, ld_m[n % 2])
            need(dve, dve_misc)
            need(dve, pe_s1)
            for t in range(TT):
                dve_misc.did(dve.tensor_scalar(Bq[n % 3][:, t], min_[n % 2][:, t], padB[:, n * TT + t:n * TT + t + 1],
                                               -BIG, ALU.mult, ALU.add))
            need(dve, dve_misc)
            need(dve, pool_xb)
            dve_misc.did(dve.tensor_reduce(free_[:], Bq[n % 3][:], AX.X, ALU.max))
            need(dve, dve_misc)
            dve_misc.did(dve.tensor_scalar(free_[:], free_[:], 0.0, None, ALU.is_ge))
            need(dve, dve_misc)
            dve_misc.did(dve.reciprocal(free_[:], free_[:]))
            need(dve, dve_misc)
            dve_misc.did(dve.tensor_tensor(nanb[:], free_[:], free_[:], ALU.subtract))
            b = misc()
            need(pe, c_dve)
            for k in range(TT):
                for t in range(TT):
                    i = pe.transpose(b[:].bitcast(BF16)[:, k * L + t * P:k * L + (t + 1) * P],
                                     Bq[n % 3][:, t, k * P:(k + 1) * P], identb[:])
            pe_misc.did(i)
            need(dve, pe_misc)
            need(dve, pe_s2)
            dve_misc.did(dve.tensor_copy(Bk[n % 3][:].rearrange("p k l -> p (k l)"), b[:].bitcast(BF16)[:, 0:TT * L]))
            need(pool, dve_misc)
            for t in range(TT):
                pool_xb.did(pool.tensor_scalar(xb[n % 4][:, t], xb[n % 4][:, t], nanb[:, t:t + 1], None, ALU.add))

        def pre_rows(n):
            need(dve, pool_ln)
            need(dve, pe_misc)
            for t in range(TT):
                dve_ln.did(dve.tensor_scalar(xn[:, t], xin[n % 3][:, t], mv[:, t, 0:1], rstd[:, t:t + 1],
                                             ALU.subtract, ALU.mult))

        def turn_rows(src, hi, lo, ready):
            b = misc()
            for r in ready:
                need(pe, r)
            for kc in range(KC):
                for t in range(TT):
                    i = pe.transpose(b[:, kc * L + t * P:kc * L + t * P + P], src[:, t, kc * P:(kc + 1) * P], ident[:])
            pe_misc.did(i)
            parts(b[:].rearrange("p (k l) -> p k l", k=KC), hi, lo)

        def pre_xT(n):
            turn_rows(xn, xT[0][:], xT[1][:], [dve_ln])

        def pre_cT(n):
            turn_rows(cin[n % 2], cT[0][:], cT[1][:], [ld_c[n % 2]])

        def product(o, lhs, rhs, last_stop=True):
            terms = [(lhs[a], rhs[c], kc) for kc in range(KC) for a, c in ((0, 0), (0, 1), (1, 0))]
            for j, (l, r, kc) in enumerate(terms):
                i = pe.matmul(o, l(kc), r(kc), start=(j == 0), stop=(j == len(terms) - 1))
            return i

        def proj(n, w, src, m0):
            b = misc()
            need(pe, act_misc)
            need(pe, dve_misc)
            for m in range(m0, m0 + 2):
                i = product(b[:, (m - m0) * L:(m - m0 + 1) * L],
                            [lambda kc, m=m, q=q: w[q][:, kc, m * P:(m + 1) * P] for q in range(2)],
                            [lambda kc, q=q: src[q][:, kc, :] for q in range(2)])
            pe_misc.did(i)
            return b

        def pre_q(n, m0):
            b = proj(n, WqT, xT, m0)
            need(act, pe_misc)
            act_misc.did(act.activation(Qh[:], b[:], ACT.Copy))
            need(dve, act_misc)
            need(dve, pe_s2)
            need(dve, c_dve)
            dve_misc.did(dve.scalar_tensor_tensor(Qm[n % 3][:, m0:m0 + 2].rearrange("p m l -> p (m l)"),
                                                  Qh[:].bitcast(F32), neglo[:], b[:], ALU.mult, ALU.add))

        def pre_k(n, m0):
            b = proj(n, WkT, cT, m0)
            need(act, pe_s2)
            need(dve, pe_s2)
            parts(b[:], K1[n % 3][:, m0:m0 + 2].rearrange("p m l -> p (m l)"),
                  K2[n % 3][:, m0:m0 + 2].rearrange("p m l -> p (m l)"))

        def pre_v(n):
            b = misc()
            for t in range(TT):
                i = product(b[:, t * E:(t + 1) * E],
                            [lambda kc, t=t, q=q: cT[q][:, kc, t * P:(t + 1) * P] for q in range(2)],
                            [lambda kc, q=q: WvT[q][:, kc, :] for q in range(2)])
            pe_misc.did(i)
            need(act, pe_misc)
            need(act, pe_pv)
            act_misc.did(act.activation(V[n % 3][:, :, :, 0:D], b[:].rearrange("p (t h d) -> p t h d", t=TT, d=D),
                                        ACT.Copy))

        def scores_for_max(n, h):
            j, m = h % HPT, h // HPT
            r = slice(j * STRIP, (j + 1) * STRIP)
            b = s1_bank[h % 2]
            need(pe, dve_misc)
            need(pe, act_misc)
            need(pe, dve_max, dve_max.count - 1 if dve_max.count > 1 else 0)
            pe.matmul(b[:], identb[:], Bq[n % 3][:].rearrange("p t l -> p (t l)"), start=True, stop=False)
            for t in range(TT):
                for i, k in enumerate((K1, K2)):
                    ins = pe.matmul(b[:, t * L:(t + 1) * L], Qm[n % 3][r, m, t * P:(t + 1) * P], k[n % 3][r, m, :],
                                    start=False, stop=(i == 1 and t == TT - 1))
            pe_s1.did(ins)
            need(dve, pe_s1)
            dve_max.did(dve.tensor_reduce(nmax[n % 2][:, h, :], b[:].rearrange("p (t k) -> p t k", t=TT), AX.X,
                                          ALU.max, negate=True))

        def max_rows(n):
            nm = nmax[n % 2][:].rearrange("p h (t o) -> p t o h", o=1).to_broadcast([P, TT, HPT, H])
            hi, lo = mrep[:, :, :, 0, :], mrep[:, :, :, 1, :]
            need(dve, dve_max)
            need(dve, pe_misc)
            dve_misc.did(dve.tensor_copy(hi.bitcast(F32R), nm))
            need(dve, dve_misc)
            dve_misc.did(dve.tensor_tensor(lo.bitcast(F32R), nm, hi, ALU.subtract))
            b = misc()
            need(pe, dve_misc)
            for t in range(TT):
                i = pe.transpose(b[:, t * P:(t + 1) * P], mrep[:, t].rearrange("p s c h -> p (s c h)"), ident[:])
            pe_misc.did(i)
            need(dve, pe_misc)
            need(dve, pe_s2)
            dve_misc.did(dve.tensor_copy(mT[n % 2][:], b[:, 0:L]))

        def scores(n, h):
            j, m = h % HPT, h // HPT
            r = slice(j * STRIP, (j + 1) * STRIP)
            b = s2_bank[h % 2]
            need(pe, act_exp, act_exp.count - 1 if act_exp.count > 1 else 0)
            need(pe, dve_misc)
            need(pe, c_dve)
            pe.matmul(b[:], identb[:], Bk[n % 3][:].rearrange("p t l -> p (t l)"), start=True, stop=False)
            for t in range(TT):
                o = b[:, t * L:(t + 1) * L]
                pe.matmul(o, K1[n % 3][r, m, t * P:(t + 1) * P], Qm[n % 3][r, m, :], start=False, stop=False)
                pe.matmul(o, K2[n % 3][r, m, t * P:(t + 1) * P], Qm[n % 3][r, m, :], start=False, stop=False)
                ins = pe.matmul(o, sel[r, h, :], mT[n % 2][r, :], start=False, stop=(t == TT - 1))
            pe_s2.did(ins)
            need(act, pe_s2)
            need(act, pe_pv)
            act_exp.did(act.activation(prob[act_exp.count % 3][:].rearrange("p t l -> p (t l)"), b[:], ACT.Exp,
                                       scale=SCALE))

        def weighted(n, h):
            j, quad = h % HPT, h // HPT
            b = pv_bank[quad % 2]
            r = slice(j * STRIP, (j + 1) * STRIP)
            g = n * H + h
            need(pe, act_exp, g + 1)
            need(pe, act_misc)
            need(pe, pool_v)
            if j == 0:
                need(pe, dve_ot)
            for t in range(TT):
                ins = pe.matmul(b[r, 0:L], V[n % 3][:, t, h, :], prob[g % 3][:, t, :], start=(t == 0),
                                stop=(t == TT - 1))
            pe_pv.did(ins)
            if j == HPT - 1:
                need(dve, pe_pv)
                need(dve, pe_misc)
                dve_ot.did(dve.tensor_copy(OT[quad][:], b[:, 0:L]))

        def post_o(n, t):
            b = misc()
            need(pe, dve_ot)
            for q in range(MQ):
                i = pe.transpose(b[:, q * P:(q + 1) * P], OT[q][:, t * P:(t + 1) * P], ident[:])
            pe_misc.did(i)
            need(dve, pe_misc)
            v = b[:].rearrange("p (h c) -> p h c", c=STRIP)
            need(dve, dve_misc)
            dve_misc.did(dve.reciprocal(rden[:], v[:, :, D]))
            need(dve, dve_misc)
            dve_misc.did(dve.tensor_tensor(ao[:, t].rearrange("p (h d) -> p h d", d=D), v[:, :, 0:D],
                                           rden[:].rearrange("p (h o) -> p h o", o=1).to_broadcast([P, H, D]),
                                           ALU.mult))

        def post_aT(n):
            turn_rows(ao, aT[0][:], aT[1][:], [dve_misc])

        def post_wo(n):
            b = misc()
            for t in range(TT):
                i = product(b[:, t * E:(t + 1) * E],
                            [lambda kc, t=t, q=q: aT[q][:, kc, t * P:(t + 1) * P] for q in range(2)],
                            [lambda kc, q=q: WoT[q][:, kc, :] for q in range(2)])
            pe_misc.did(i)
            need(dve, pe_misc)
            need(dve, pool_xb)
            rows = x2[:, n * TT:(n + 1) * TT]
            dve_misc.did(dve.tensor_tensor(rows, b[:].rearrange("p (t e) -> p t e", t=TT), xb[n % 4][:], ALU.add))
            need(dve, dve_misc)
            for t in range(TT):
                dve_ln.did(dve.bn_stats(st6b[:, t], x2[:, n * TT + t]))
            need(dve, dve_ln)
            need(dve, pool_ln)
            for t in range(TT):
                dve_ln.did(dve.bn_aggr(mvb[:, t], st6b[:, t]))
            need(pool, dve_ln)
            pool_ln.did(pool.tensor_scalar(veb[:], mvb[:, :, 1], LN_EPS, None, ALU.add))
            need(pool, pool_ln)
            pool_ln.did(pool.tensor_tensor(rstdb[:], veb[:], half[:], ALU.pow))

        def post_rows(n):
            need(dve, pool_ln)
            need(dve, pe_misc)
            for t in range(TT):
                dve_ln.did(dve.tensor_scalar(x2n[:, t], x2[:, n * TT + t], mvb[:, t, 0:1], rstdb[:, t:t + 1],
                                             ALU.subtract, ALU.mult))

        def post_xT(n):
            c = slice(n * L, (n + 1) * L)
            turn_rows(x2n, XTh[:, :, c], XTl[:, :, c], [dve_ln])

        def post_gate(n):
            b = misc()
            for t in range(TT):
                c = slice((n * TT + t) * P, (n * TT + t + 1) * P)
                k = 0
                for kc in range(KC):
                    for xt in (XTh, XTl):
                        for w in WgT:
                            i = pe.matmul(b[:, t * NE:(t + 1) * NE], xt[:, kc, c], w[:, kc, :], start=(k == 0),
                                          stop=(k == 4 * KC - 1))
                            k += 1
            pe_misc.did(i)
            need(dve, pe_misc)
            dve_misc.did(dve.tensor_copy(logits[:, n * TT:(n + 1) * TT],
                                         b[:, 0:TT * NE].rearrange("p (t e) -> p t e", e=NE)))

        def pieces_before(n):
            return [lambda: pre_norm(n), lambda: pre_mask(n), lambda: pre_rows(n), lambda: pre_cT(n), lambda: pre_xT(n),
                    lambda: pre_k(n, 0), lambda: pre_k(n, 2), lambda: pre_q(n, 0), lambda: pre_q(n, 2),
                    lambda: pre_v(n)]

        def pieces_after(n):
            return [lambda: post_o(n, 0), lambda: post_o(n, 1), lambda: post_aT(n), lambda: post_wo(n),
                    lambda: post_rows(n), lambda: post_xT(n), lambda: post_gate(n)]

        for f in pieces_before(0):
            f()
        for h in range(H):
            scores_for_max(0, h)
        max_rows(0)
        for f in pieces_before(1):
            f()
        for n in range(NB):
            if n + 2 < NB:
                load(n + 2)
            before = pieces_before(n + 2) if n + 2 < NB else []
            after = pieces_after(n - 1) if n else []
            for h in range(H):
                if n + 1 < NB:
                    scores_for_max(n + 1, h)
                scores(n, h)
                if h:
                    weighted(n, h - 1)
                todo = after if h < 8 else before
                if h % 8 == 0 and h == 8:
                    for f in after:
                        f()
                    after = []
                if todo:
                    todo.pop(0)()
            weighted(n, H - 1)
            for f in after + before:
                f()
            if n + 1 < NB:
                max_rows(n + 1)
        for f in pieces_after(NB - 1):
            f()

        A.close()
        for engine in (sp, act, dve, pe, pool):
            for stage in (pe_misc, dve_misc, act_misc, pe_pv, pe_s2, act_exp, dve_ln, pool_ln, pool_xb):
                need(engine, stage)
        g = ExitStack()
        gd = step("gd")
        ga = step("ga")
        mx = sb(g, "mx", [P, NT])
        pr = sb(g, "pr", [P, NT, NE])
        sm = sb(g, "sm", [P, NT])
        less = sb(g, "less", [P, NE, NE])
        gt = sb(g, "gt", [P, NT, NE, NE])
        eq = sb(g, "eq", [P, NT, NE, NE])
        rank = sb(g, "rank", [P, NT, NE])
        gp = step("gp")
        gp.did(pool.memset(less[:], 1.0))
        need(pool, gp)
        gp.did(pool.affine_select(out=less[:], in_=less[:], compare_op=ALU.is_gt, fill=0.0, base=0,
                                  pattern=[[1, NE], [-1, NE]], channel_multiplier=0))
        need(dve, dve_misc)
        gd.did(dve.tensor_reduce(mx[:], logits[:], AX.X, ALU.max))
        need(dve, gd)

        def over(v, shape):
            return v.rearrange("p t (o e) -> p t o e", o=1).to_broadcast(shape)

        gd.did(dve.tensor_tensor(pr[:], logits[:], mx[:].rearrange("p (t o) -> p t o", o=1).to_broadcast([P, NT, NE]),
                                 ALU.subtract))
        need(act, gd)
        ga.did(act.activation(pr[:], pr[:], ACT.Exp))
        need(dve, ga)
        gd.did(dve.tensor_reduce(sm[:], pr[:], AX.X, ALU.add))
        need(dve, gd)
        gd.did(dve.reciprocal(sm[:], sm[:]))
        need(dve, gd)
        gd.did(dve.tensor_tensor(pr[:], pr[:], sm[:].rearrange("p (t o) -> p t o", o=1).to_broadcast([P, NT, NE]),
                                 ALU.mult))
        need(dve, gd)
        full = [P, NT, NE, NE]
        for t in range(NT):
            pj = pr[:, t].rearrange("p (o e) -> p o e", o=1).to_broadcast([P, NE, NE])
            pi = pr[:, t].rearrange("p (e o) -> p e o", o=1).to_broadcast([P, NE, NE])
            gd.did(dve.tensor_tensor(gt[:, t], pj, pi, ALU.is_gt))
            gd.did(dve.tensor_tensor(eq[:, t], pj, pi, ALU.is_equal))
        need(dve, gd)
        need(dve, gp)
        for t in range(NT):
            gd.did(dve.tensor_tensor(eq[:, t], eq[:, t], less[:], ALU.mult))
        need(dve, gd)
        gd.did(dve.tensor_tensor(gt[:], gt[:], eq[:], ALU.add))
        need(dve, gd)
        gd.did(dve.tensor_reduce(rank[:], gt[:].rearrange("p t e j -> p (t e) j"), AX.X, ALU.add))
        need(dve, gd)
        gd.did(dve.tensor_scalar(rank[:], rank[:], 2.0, None, ALU.is_lt))
        need(dve, gd)
        gd.did(dve.tensor_tensor(cw[:], rank[:], pr[:], ALU.mult))
        g.close()

        B = ExitStack()
        CH = 512
        NCH = NT * P // CH
        MF = F // P
        w_in = [sb(B, f"w_in{i}", [P, 4, 512]) for i in range(2)]
        W1p = [sb(B, f"W1p{i}", [P, KC, F], F32R) for i in range(2)]
        W2p = [sb(B, f"W2p{i}", [P, MF, E], F32R) for i in range(2)]
        hf = [sb(B, f"hf{i}", [P, CH]) for i in range(2)]
        hh = [sb(B, f"hh{i}", [P, MF, CH], F32R) for i in range(2)]
        hl = [sb(B, f"hl{i}", [P, MF, CH], F32R) for i in range(2)]
        hb = [B.enter_context(nc.psum_tensor(f"hb{i}", [P, CH], F32)) for i in range(4)]
        yb = [B.enter_context(nc.psum_tensor(f"yb{i}", [P, 512], F32)) for i in range(4)]

        ld_e = [step(f"ld_e{i}", 16) for i in range(2)]
        split1 = step("split1")
        split2 = step("split2")
        pe_h = step("pe_h")
        act_g = step("act_g")
        dve_h = step("dve_h")
        pe_y = step("pe_y")
        dve_y = step("dve_y")
        prev_sp = step("prev_sp")
        W1_d = W1.rearrange("e (k p) f -> e p k f", p=P)
        W2_d = W2.rearrange("e (m p) d -> e p m d", p=P)
        for st in (gd, ga, gp):
            for eng in (sp, act, dve, pe, pool):
                need(eng, st)

        def weights(e):
            for q in range(4):
                w = w_in[q % 2]
                need(sp, split1)
                need(sp, split2)
                if q < 2:
                    src, dst, st = W1_d[e, :, q, :], [a[:, q, :] for a in W1p], split1
                    v = w[:].rearrange("p a b -> p (a b)")[:, 0:F]
                else:
                    c = slice((q - 2) * MF // 2, (q - 1) * MF // 2)
                    src, dst, st = W2_d[e, :, c, :], [a[:, c, :] for a in W2p], split2
                    v = w[:].rearrange("p a b -> p (a b)")[:, 0:F].rearrange("p (m d) -> p m d", d=E)
                ld_e[q % 2].did(sp.dma_start(v, src))
                need(dve, ld_e[q % 2])
                need(dve, pe_h)
                need(dve, pe_y)
                st.did(dve.tensor_copy(dst[0], v))
                need(dve, st)
                st.did(dve.tensor_tensor(dst[1], v, dst[0].bitcast(F32), ALU.subtract))

        nh = 0
        for e in range(NE):
            weights(e)
            for c in range(NCH):
                tok = slice(c * CH, (c + 1) * CH)
                need(pe, split1)
                for m in range(MF):
                    b = hb[nh % 4]
                    need(pe, act_g, max(act_g.count - 3, 0))
                    terms = [(kc, a, x_) for kc in range(KC) for a, x_ in ((0, XTh), (1, XTh), (0, XTl))]
                    for i, (kc, a, x_) in enumerate(terms):
                        ins = pe.matmul(b[:], W1p[a][:, kc, m * P:(m + 1) * P], x_[:, kc, tok], start=(i == 0),
                                        stop=(i == len(terms) - 1))
                    pe_h.did(ins)
                    need(act, pe_h)
                    need(act, dve_h, max(dve_h.count - 2, 0))
                    act_g.did(act.activation(hf[nh % 2][:], b[:], ACT.Gelu, bias=b1T[:, e * MF + m:e * MF + m + 1]))
                    need(dve, act_g)
                    need(dve, pe_y, max(pe_y.count - CH // P, 0))
                    dve_h.did(dve.tensor_copy(hh[c % 2][:, m], hf[nh % 2][:]))
                    need(dve, dve_h)
                    dve_h.did(dve.tensor_tensor(hl[c % 2][:, m], hf[nh % 2][:], hh[c % 2][:, m].bitcast(F32),
                                                ALU.subtract))
                    nh += 1
                need(pe, dve_h)
                need(pe, split2)
                for t in range(CH // P):
                    b = yb[t][:, 0:E]
                    tc_ = slice(t * P, (t + 1) * P)
                    need(pe, dve_y, max(dve_y.count - 3, 0))
                    pe.matmul(b, ones2[:], b2r[:, e, :], start=True, stop=False)
                    for m in range(MF):
                        pe.matmul(b, hh[c % 2][:, m, tc_], W2p[0][:, m, :], start=False, stop=False)
                        pe.matmul(b, hh[c % 2][:, m, tc_], W2p[1][:, m, :], start=False, stop=False)
                        ins = pe.matmul(b, hl[c % 2][:, m, tc_], W2p[0][:, m, :], start=False, stop=(m == MF - 1))
                    pe_y.did(ins)
                    T = c * (CH // P) + t
                    need(dve, pe_y)
                    need(dve, dve_y)
                    dve_y.did(dve.scalar_tensor_tensor(x2[:, T], b, cw[:, T, e:e + 1], x2[:, T], ALU.mult, ALU.add))
        need(sp, dve_y)
        for k in range(4):
            q = NT // 4
            st_out.did(sp.dma_start(out_d[:, k * q:(k + 1) * q], x2[:, k * q:(k + 1) * q]))
        need(sp, st_out)
        B.close()


def kernel(x, ctx_1024, mask_BxS2_bf1, mask_BxSxS2_bf1, L0_xattn_Wq, L0_xattn_Wk, L0_xattn_Wv, L0_xattn_Wo,
           L0_xattn_bo, L0_ffn_w_gate, L0_ffn_W1, L0_ffn_b1, L0_ffn_W2, L0_ffn_b2):
    import concourse.bacc as bacc
    from concourse.bass_utils import run_bass_kernel_spmd

    named = dict(x=x, ctx_in=ctx_1024, pad=mask_BxS2_bf1, mask=mask_BxSxS2_bf1, Wq=L0_xattn_Wq, Wk=L0_xattn_Wk, Wv=L0_xattn_Wv, Wo=L0_xattn_Wo,
                 bo=L0_xattn_bo, w_gate=L0_ffn_w_gate, W1=L0_ffn_W1, b1=L0_ffn_b1, W2=L0_ffn_W2, b2=L0_ffn_b2)
    nc = bacc.Bacc("TRN2", target_bir_lowering=False, num_devices=1)
    arrays, args = {}, {}
    for name, a in named.items():
        a = np.ascontiguousarray(a)
        if a.dtype == bool:
            a = a.view(np.uint8)
        arrays[f"in_{name}"] = a
        args[name] = nc.dram_tensor(f"in_{name}", a.shape, mybir.dt.from_np(a.dtype), kind="ExternalInput").ap()
    out = nc.dram_tensor("out_0", np.shape(x), F32, kind="ExternalOutput").ap()
    build(nc, out=out, **args)
    r = run_bass_kernel_spmd(nc, [arrays], core_ids=[0])
    return r.results[0]["out_0"]
```

```python
from contextlib import ExitStack

import numpy as np
import concourse.bass as bass
from concourse import mybir

F32 = mybir.dt.float32
F32R = mybir.dt.float32r
BF16 = mybir.dt.bfloat16
U8 = mybir.dt.uint8
I32 = mybir.dt.int32
ALU = mybir.AluOpType
ACT = mybir.ActivationFunctionType
AX = mybir.AxisListType

P = 128
LN_EPS = 1e-5
BIG = 2.0 ** 100
FAR = 2.0 ** 17


class Step:

    def __init__(self, ctx, nc, name, by=1):
        self.sem, self.by, self.count, self.waited = ctx.enter_context(nc.semaphore(name)), by, 0, {}

    def did(self, instruction):
        instruction.then_inc(self.sem, self.by)
        self.count += self.by


def need(engine, step, count=None):
    count = step.count if count is None else count
    if count > step.waited.get(engine, 0):
        engine.wait_ge(step.sem, count)
        step.waited[engine] = count


def build(nc, x, ctx_in, pad, mask, Wq, Wk, Wv, Wo, bo, w_gate, W1, b1, W2, b2, out):
    pe, dve, act, pool, sp = nc.tensor, nc.vector, nc.scalar, nc.gpsimd, nc.sync
    NB, L, E = x.shape
    NE, _, F = W1.shape
    D = 16
    H = E // D
    TT = L // P
    KC = E // P
    NT = NB * TT
    HALF = 4 * D
    MQ = H * HALF // P
    MF = F // P
    OQ = 4
    OS = P // OQ
    SCALE = 1.0 / float(np.sqrt(D))
    TS = 256
    TOP = 2
    REGION = NT * P + TS
    EXTRA = (TOP * NT * P - NE) // TS
    NTILE = NE + EXTRA
    MORE = NT * P // TS - 1
    assert TT == 2 and KC == 2 and H == 16 and MQ == 8

    x_d = x.rearrange("n (t p) e -> n p t e", p=P)
    c_d = ctx_in.rearrange("n (t p) e -> n p t e", p=P)
    m_d = mask.rearrange("n (t p) k -> n p t k", p=P)
    out_d = out.rearrange("n (t p) e -> p (n t) e", p=P)
    lists = nc.dram_tensor("lists", [NE * REGION, E], F32, kind="Internal").ap()
    results = nc.dram_tensor("results", [NTILE * TS, E], F32, kind="Internal").ap()

    top = ExitStack()
    with top:
        def step(name, by=1):
            return Step(top, nc, name, by)

        def sb(ctx, name, shape, dt=F32):
            return ctx.enter_context(nc.sbuf_tensor(name, shape, dt))

        ident = sb(top, "ident", [P, P])
        x2 = sb(top, "x2", [P, NT, E])
        b1T = sb(top, "b1T", [P, NE * MF])
        less = sb(top, "less", [P, NE, NE])
        base = sb(top, "base", [P, NE])
        place = sb(top, "place", [P, NT, NE])
        chosen = sb(top, "chosen", [P, NT, NE], BF16)
        weight = sb(top, "weight", [P, NT, NE])
        run = sb(top, "run", [P, NE], BF16)
        onesb = sb(top, "onesb", [P, P], BF16)
        zero = sb(top, "zero", [P, TS // P, E])
        w1_in = [sb(top, "w1_in0", [P, KC, F])]
        w2_in = [sb(top, "w2_in0", [P, MF, E])]

        A = ExitStack()
        bank = [A.enter_context(nc.psum_tensor(f"bank{i}", [P, 512], F32)) for i in range(8)]
        s1_bank, s2_bank, pv_bank = bank[0:2], bank[2:4], bank[4]
        MISC = (5, 6, 7)

        WqT = [sb(A, f"WqT{i}", [P, KC, MQ * P], F32R) for i in range(2)]
        WkT = [sb(A, f"WkT{i}", [P, KC, MQ * P], F32R) for i in range(2)]
        WvT = [sb(A, f"WvT{i}", [P, KC, E], F32R) for i in range(2)]
        WoT = [sb(A, f"WoT{i}", [P, KC, E], F32R) for i in range(2)]
        WgT = [sb(A, f"WgT{i}", [P, KC, NE], F32R) for i in range(2)]
        bo_b = sb(A, "bo_b", [P, E])
        padB = sb(A, "padB", [P, NT])
        identb = sb(A, "identb", [P, P], BF16)
        before = sb(A, "before", [P, P], BF16)
        neglo_q = sb(A, "neglo_q", [P, 1])
        neglo_k = sb(A, "neglo_k", [P, 1])
        sel = sb(A, "sel", [P, H, P], F32R)
        half = sb(A, "half", [P, TT])
        xin = [sb(A, f"xin{i}", [P, TT, E]) for i in range(2)]
        cin = [sb(A, f"cin{i}", [P, TT, E]) for i in range(2)]
        min_ = [sb(A, f"min{i}", [P, TT, L], U8) for i in range(2)]
        stats = [sb(A, f"stats{i}", [P, TT, 6]) for i in range(2)]
        mv = [sb(A, f"mv{i}", [P, TT, 2]) for i in range(2)]
        ve = [sb(A, f"ve{i}", [P, TT]) for i in range(2)]
        rstd = [sb(A, f"rstd{i}", [P, TT]) for i in range(2)]
        free_ = sb(A, "free_", [P, TT])
        nanb = sb(A, "nanb", [P, TT])
        Bq = [sb(A, f"Bq{i}", [P, TT, L], BF16) for i in range(3)]
        Bk = [sb(A, f"Bk{i}", [P, TT, L], BF16) for i in range(3)]
        Q = [sb(A, f"Q{i}", [P, MQ, L], F32R) for i in range(3)]
        K = [sb(A, f"K{i}", [P, MQ, L], F32R) for i in range(3)]
        V = [sb(A, f"V{i}", [P, TT, H, OS]) for i in range(3)]

        first = ExitStack()
        Wst = sb(first, "Wst", [P, 4, TT, E])
        wg_in = sb(first, "wg_in", [NE, E])
        b1_in = sb(first, "b1_in", [NE * MF, P])
        pad_in = sb(first, "pad_in", [NT, P], U8)
        pad_f = sb(first, "pad_f", [NT, P])
        rows16 = sb(first, "rows16", [P, D])
        rowsm = sb(first, "rowsm", [P, 1])

        ld_w = step("ld_w", 16)
        ld_x = [step(f"ld_x{i}", 16) for i in range(2)]
        ld_c = [step(f"ld_c{i}", 16) for i in range(2)]
        ld_m = [step(f"ld_m{i}", 16) for i in range(2)]
        ld_w1 = [step(f"ld_w1{i}", 16) for i in range(2)]
        ld_w2 = [step(f"ld_w2{i}", 16) for i in range(2)]
        st_list = step("st_list", 16)
        st_zero = step("st_zero", 16)
        pool_c = step("pool_c")
        dve_c = step("dve_c")
        pe_misc, act_misc, dve_misc = step("pe_misc"), step("act_misc"), step("dve_misc")
        pe_s1, dve_max = step("pe_s1"), step("dve_max")
        pe_s2, act_exp = step("pe_s2"), step("act_exp")
        pe_pv, dve_ot = step("pe_pv"), step("dve_ot")
        dve_ln, pool_ln, pool_x2 = step("dve_ln"), step("pool_ln"), step("pool_x2")
        dve_gate, act_gate = step("dve_gate"), step("act_gate")

        for i, w in enumerate((Wq, Wk, Wv, Wo)):
            ld_w.did(sp.dma_start(Wst[:, i], w.rearrange("(t p) e -> p t e", p=P)))
        ld_w.did(act.dma_start(pad_in[:], pad.rearrange("n (t p) -> (n t) p", p=P)))
        ld_w.did(act.dma_start(wg_in[:], w_gate))
        ld_w.did(act.dma_start(b1_in[:], b1.rearrange("e (m p) -> (e m) p", p=P)))
        ld_w.did(act.dma_start(bo_b[:], bo.rearrange("(o e) -> o e", o=1).to_broadcast([P, E])))

        def load(n):
            need(sp, dve_ln)
            need(sp, pool_x2)
            need(sp, pe_misc)
            need(sp, dve_misc)
            ld_c[n % 2].did(sp.dma_start(cin[n % 2][:], c_d[n]))
            ld_x[n % 2].did(sp.dma_start(xin[n % 2][:], x_d[n]))
            ld_m[n % 2].did(sp.dma_start(min_[n % 2][:], m_d[n]))

        load(0)
        load(1)

        pool_c.did(pool.memset(ident[:], 0.0))
        pool_c.did(pool.memset(half[:], -0.5))
        pool_c.did(pool.memset(less[:], 1.0))
        pool_c.did(pool.memset(before[:], 1.0))
        pool_c.did(pool.memset(onesb[:], 1.0))
        pool_c.did(pool.memset(run[:], 0.0))
        pool_c.did(pool.memset(zero[:], 0.0))
        for e in range(NE):
            pool_c.did(pool.memset(base[:, e:e + 1], float(e * REGION)))
        need(pool, pool_c)
        pool_c.did(pool.affine_select(out=ident[:], in_=ident[:], compare_op=ALU.not_equal, fill=1.0, base=0,
                                      pattern=[[-1, P]], channel_multiplier=1))
        pool_c.did(pool.affine_select(out=less[:], in_=less[:], compare_op=ALU.is_gt, fill=0.0, base=0,
                                      pattern=[[1, NE], [-1, NE]], channel_multiplier=0))
        pool_c.did(pool.affine_select(out=before[:], in_=before[:], compare_op=ALU.is_gt, fill=0.0, base=0,
                                      pattern=[[1, P]], channel_multiplier=-1))
        for i in range(3):
            pool_c.did(pool.memset(V[i][:, :, :, D:], 0.0))
        need(pool, pool_c)
        for i in range(3):
            pool_c.did(pool.memset(V[i][:, :, :, D:D + 1], 1.0))
        need(sp, pool_c)
        for e in range(NE):
            st_zero.did(sp.dma_start(lists[e * REGION:e * REGION + TS, :].rearrange("(t p) e -> p t e", p=P), zero[:]))
        ld_w1[0].did(sp.dma_start(w1_in[0][:], W1[0].rearrange("(k p) f -> p k f", p=P)))
        ld_w2[0].did(sp.dma_start(w2_in[0][:], W2[0].rearrange("(m p) d -> p m d", p=P)))

        need(dve, pool_c)
        i4 = ident[:].rearrange("p (a c d) -> p a c d", c=4, d=D)
        dve_c.did(dve.tensor_reduce(rows16[:], ident[:].rearrange("p (a h) -> p h a", h=D), AX.X, ALU.add))
        dve_c.did(dve.tensor_reduce(neglo_q[:], ident[:].rearrange("p (s h) -> p s h", h=2 * D)[:, :, D:], AX.XY,
                                    ALU.add, negate=True))
        dve_c.did(dve.tensor_reduce(neglo_k[:], i4[:, :, 2:4, :].rearrange("p a c d -> p a (c d)"), AX.XY,
                                    ALU.add, negate=True))
        dve_c.did(dve.tensor_reduce(rowsm[:], i4[:, :, 0:2, :].rearrange("p a c d -> p a (c d)"), AX.XY, ALU.add))
        dve_c.did(dve.tensor_copy(identb[:], ident[:]))
        need(dve, dve_c)
        dve_c.did(dve.tensor_scalar(sel[:], rows16[:].rearrange("p (h o) -> p h o", o=1).to_broadcast([P, H, P]),
                                    rowsm[:], None, ALU.mult))
        need(dve, ld_w)
        dve_c.did(dve.tensor_copy(pad_f[:], pad_in[:]))

        readers = {b: () for b in MISC}
        turns = list(MISC)

        def take():
            b = turns.pop(0)
            for stage, count in readers[b]:
                need(pe, stage, count)
            return b

        def claim():
            while not turns:
                yield
            return take()

        def give(b):
            readers[b] = ((act_misc, act_misc.count), (dve_misc, dve_misc.count))
            turns.append(b)

        def parts(src, hi, lo):
            need(act, pe_misc)
            act_misc.did(act.activation(hi, src, ACT.Copy))
            need(dve, act_misc)
            dve_misc.did(dve.tensor_tensor(lo, src, hi.bitcast(F32), ALU.subtract))

        need(pe, ld_w)
        need(pe, pool_c)
        need(pe, dve_c)
        for i in range(4):
            b = take()
            o = bank[b]
            for kc in range(KC):
                for fc in range(TT):
                    t = pe.transpose(o[:, kc * E + fc * P:kc * E + fc * P + P], Wst[:, i, fc, kc * P:kc * P + P],
                                     ident[:])
            pe_misc.did(t)
            if i < 2:
                for kc in range(KC):
                    src = o[:, kc * E:(kc + 1) * E].rearrange("p (h d) -> p h d", d=D)
                    hi, lo = (w[:, kc, :].rearrange("p (h c d) -> p h c d", c=4, d=D) for w in (WqT, WkT)[i])
                    need(act, dve_misc)
                    parts(src, hi[:, :, 0, :], lo[:, :, 0, :])
                    need(act, dve_misc)
                    need(dve, dve_misc)
                    for c in range(1, 4):
                        act_misc.did(act.activation(hi[:, :, c, :], src, ACT.Copy))
                        dve_misc.did(dve.tensor_copy(lo[:, :, c, :], lo[:, :, 0, :].bitcast(F32)))
            else:
                hi, lo = (WvT, WoT)[i - 2]
                parts(o[:].rearrange("p (k e) -> p k e", k=KC), hi[:], lo[:])
            give(b)
        b = take()
        o = bank[b]
        for kc in range(KC):
            pe.transpose(o[:, kc * NE:(kc + 1) * NE], wg_in[:, kc * P:(kc + 1) * P], ident[0:NE, 0:NE])
        nb1 = NE * MF
        pe.transpose(o[:, 256:256 + NT], pad_f[:], ident[0:NT, 0:NT])
        pe_misc.did(pe.transpose(o[:, 64:64 + nb1], b1_in[:], ident[0:nb1, 0:nb1]))
        parts(o[:, 0:KC * NE].rearrange("p (k e) -> p k e", k=KC), WgT[0][:], WgT[1][:])
        dve_misc.did(dve.tensor_copy(b1T[:], o[:, 64:64 + nb1]))
        dve_misc.did(dve.tensor_scalar(padB[:], o[:, 256:256 + NT], BIG, None, ALU.mult))
        give(b)
        first.close()
        for engine in (act, dve, pool):
            need(engine, pe_misc)
            need(engine, dve_misc)
            need(engine, dve_c)
        xn = sb(A, "xn", [P, TT, E])
        xT = [sb(A, f"xT{i}", [P, KC, L], F32R) for i in range(2)]
        cT = [sb(A, f"cT{i}", [P, KC, L], F32R) for i in range(2)]
        hi_t = [sb(A, f"hi_t{i}", [P, 2 * L], F32R) for i in range(2)]
        nmax = [sb(A, f"nmax{i}", [P, H, TT]) for i in range(2)]
        mrep = sb(A, "mrep", [P, TT, 2, 4, H])
        mT = [sb(A, f"mT{i}", [P, L], F32R) for i in range(2)]
        prob = [sb(A, f"prob{i}", [P, TT, L]) for i in range(3)]
        OT = [sb(A, f"OT{i}", [P, L]) for i in range(H // OQ)]
        rden = sb(A, "rden", [P, H])
        ao = sb(A, "ao", [P, TT, E])
        aT = [sb(A, f"aT{i}", [P, KC, L], F32R) for i in range(2)]
        x2n = [sb(A, f"x2n{i}", [P, TT, E]) for i in range(2)]
        yT = [sb(A, f"yT{i}", [P, KC, L], F32R) for i in range(2)]
        lg = sb(A, "lg", [P, TT, NE])
        mx = sb(A, "mx", [P, TT])
        sm = sb(A, "sm", [P, TT])
        larger = sb(A, "larger", [P, TT, NE, NE])
        equal = sb(A, "equal", [P, TT, NE, NE])
        rank = sb(A, "rank", [P, TT, NE])
        off = sb(A, "off", [P, TT, NE])
        ends = sb(A, "ends", [P, 2, TT])
        rows = [sb(A, f"rows{i}", [P, 2, TT], I32) for i in range(2)]
        pool_c.did(pool.memset(mrep[:], 0.0))

        def turn_rows(tag, src, dst, *stages):
            b = yield from claim()
            for stage in stages:
                need(pe, stage)
            for kc in range(KC):
                for t in range(TT):
                    i = pe.transpose(bank[b][:, kc * L + t * P:kc * L + t * P + P], src[:, t, kc * P:(kc + 1) * P],
                                     ident[:])
            pe_misc.did(i)
            yield
            need(act, pe_misc)
            need(dve, pe_misc)
            parts(bank[b][:].rearrange("p (k l) -> p k l", k=KC), dst[0][:], dst[1][:])
            give(b)
            turned[tag] = ((act_misc, act_misc.count), (dve_misc, dve_misc.count))

        def product(o, lhs, rhs):
            terms = [(lhs[a], rhs[c], kc) for kc in range(KC) for a, c in ((0, 0), (0, 1), (1, 0))]
            for j, (l, r, kc) in enumerate(terms):
                i = pe.matmul(o, l(kc), r(kc), start=(j == 0), stop=(j == len(terms) - 1))
            return i

        def norm(n, which, src, dst):
            need(dve, pool_ln)
            for t in range(TT):
                dve_ln.did(dve.bn_stats(stats[which][:, t], src[:, t]))
            yield
            need(dve, dve_ln)
            for t in range(TT):
                dve_ln.did(dve.bn_aggr(mv[which][:, t], stats[which][:, t]))
            need(pool, dve_ln)
            pool_ln.did(pool.tensor_scalar(ve[which][:], mv[which][:, :, 1], LN_EPS, None, ALU.add))
            need(pool, pool_ln)
            pool_ln.did(pool.tensor_tensor(rstd[which][:], ve[which][:], half[:], ALU.pow))
            here = pool_ln.count
            yield
            yield
            need(dve, pool_ln, here)
            need(dve, pe_misc)
            for t in range(TT):
                dve_ln.did(dve.tensor_scalar(dst[:, t], src[:, t], mv[which][:, t, 0:1], rstd[which][:, t:t + 1],
                                             ALU.subtract, ALU.mult))

        def norm1(n):
            need(dve, ld_x[n % 2])
            need(pool, ld_x[n % 2])
            need(pool, ld_w)
            for t in range(TT):
                pool_x2.did(pool.tensor_tensor(x2[:, n * TT + t], xin[n % 2][:, t], bo_b[:], ALU.add))
            yield from norm(n, 0, xin[n % 2], xn)

        def masks(n):
            need(dve, ld_m[n % 2])
            need(dve, pe_s1)
            for t in range(TT):
                dve_misc.did(dve.tensor_scalar(Bq[n % 3][:, t], min_[n % 2][:, t], padB[:, n * TT + t:n * TT + t + 1],
                                               -BIG, ALU.mult, ALU.add))
            yield
            need(dve, dve_misc)
            need(dve, pool_x2)
            dve_misc.did(dve.tensor_reduce(free_[:], Bq[n % 3][:], AX.X, ALU.max))
            need(pe, dve_misc)
            b = yield from claim()
            for k in range(TT):
                for t in range(TT):
                    i = pe.transpose(bank[b][:].bitcast(BF16)[:, k * L + t * P:k * L + (t + 1) * P],
                                     Bq[n % 3][:, t, k * P:(k + 1) * P], identb[:])
            pe_misc.did(i)
            need(dve, dve_misc)
            dve_misc.did(dve.tensor_scalar(free_[:], free_[:], 0.0, None, ALU.is_ge))
            yield
            need(dve, pe_misc)
            need(dve, pe_s2, max(n - 2, 0) * H)
            dve_misc.did(dve.tensor_copy(Bk[n % 3][:].rearrange("p k l -> p (k l)"),
                                         bank[b][:].bitcast(BF16)[:, 0:TT * L]))
            give(b)
            need(dve, dve_misc)
            dve_misc.did(dve.reciprocal(free_[:], free_[:]))
            yield
            need(dve, dve_misc)
            dve_misc.did(dve.tensor_tensor(nanb[:], free_[:], free_[:], ALU.subtract))
            need(pool, dve_misc)
            need(pool, pool_x2)
            for t in range(TT):
                pool_x2.did(pool.tensor_scalar(x2[:, n * TT + t], x2[:, n * TT + t], nanb[:, t:t + 1], None, ALU.add))

        def project(n, w, src, m0, dst, neglo, which):
            b = yield from claim()
            tag = ("c" if src is cT else "x", n)
            while tag not in turned:
                yield
            for stage, count in turned[tag]:
                need(pe, stage, count)
            for m in range(m0, m0 + 2):
                i = product(bank[b][:, (m - m0) * L:(m - m0 + 1) * L],
                            [lambda kc, m=m, q=q: w[q][:, kc, m * P:(m + 1) * P] for q in range(2)],
                            [lambda kc, q=q: src[q][:, kc, :] for q in range(2)])
            pe_misc.did(i)
            yield
            need(act, pe_misc)
            need(act, dve_misc)
            act_misc.did(act.activation(hi_t[which][:], bank[b][:], ACT.Copy))
            need(dve, act_misc)
            need(dve, pe_s2, max(n - 2, 0) * H)
            dve_misc.did(dve.scalar_tensor_tensor(dst[n % 3][:, m0:m0 + 2].rearrange("p m l -> p (m l)"),
                                                  hi_t[which][:].bitcast(F32), neglo[:], bank[b][:], ALU.mult,
                                                  ALU.add))
            give(b)

        def values(n):
            b = yield from claim()
            for t in range(TT):
                i = product(bank[b][:, t * E:(t + 1) * E],
                            [lambda kc, t=t, q=q: cT[q][:, kc, t * P:(t + 1) * P] for q in range(2)],
                            [lambda kc, q=q: WvT[q][:, kc, :] for q in range(2)])
            pe_misc.did(i)
            yield
            need(act, pe_misc)
            need(act, pool_c)
            need(act, pe_pv, max(n - 2, 0) * H)
            act_misc.did(act.activation(V[n % 3][:, :, :, 0:D],
                                        bank[b][:].rearrange("p (t h d) -> p t h d", t=TT, d=D), ACT.Copy))
            give(b)
            ready[n] = (act_misc.count, dve_misc.count)

        turned, ready, maxima = {}, {}, {}

        def max_rows(n):
            nm = nmax[n % 2][:].rearrange("p h (t o) -> p t o h", o=1).to_broadcast([P, TT, 2, H])
            hi, lo = mrep[:, :, :, 0, :], mrep[:, :, :, 1, :]
            need(dve, dve_max, (n + 1) * H)
            need(dve, pe_misc)
            need(dve, pool_c)
            dve_misc.did(dve.tensor_copy(hi.bitcast(F32R), nm))
            need(dve, dve_misc)
            dve_misc.did(dve.tensor_tensor(lo.bitcast(F32R), nm, hi, ALU.subtract))
            b = yield from claim()
            need(pe, dve_misc)
            for t in range(TT):
                i = pe.transpose(bank[b][:, t * P:(t + 1) * P], mrep[:, t].rearrange("p a c h -> p (a c h)"), ident[:])
            pe_misc.did(i)
            yield
            need(dve, pe_misc)
            need(dve, pe_s2, max(n - 1, 0) * H)
            dve_misc.did(dve.tensor_copy(mT[n % 2][:], bank[b][:, 0:L]))
            give(b)
            maxima[n] = dve_misc.count

        def head(g):
            n, h = divmod(g, H)
            return n, h, slice((h % 2) * HALF, (h % 2 + 1) * HALF), h // 2

        def scores_for_max(g):
            n, h, r, m = head(g)
            b = s1_bank[g % 2]
            need(pe, act_misc, ready[n][0])
            need(pe, dve_misc, ready[n][1])
            need(pe, dve_max, max(g - 1, 0))
            pe.matmul(b[:], identb[:], Bq[n % 3][:].rearrange("p t l -> p (t l)"), start=True, stop=False)
            for t in range(TT):
                i = pe.matmul(b[:, t * L:(t + 1) * L], Q[n % 3][r, m, t * P:(t + 1) * P], K[n % 3][r, m, :],
                              start=False, stop=(t == TT - 1))
            pe_s1.did(i)

        def take_max(g):
            n, h, _, _ = head(g)
            need(dve, pe_s1, g + 1)
            if h == 0:
                need(dve, dve_misc)
            dve_max.did(dve.tensor_reduce(nmax[n % 2][:, h, :], s1_bank[g % 2][:].rearrange("p (t k) -> p t k", t=TT),
                                          AX.X, ALU.max, negate=True))

        def scores(g):
            n, h, r, m = head(g)
            b = s2_bank[g % 2]
            need(pe, act_exp, max(g - 1, 0))
            need(pe, dve_misc, maxima[n])
            pe.matmul(b[:], identb[:], Bk[n % 3][:].rearrange("p t l -> p (t l)"), start=True, stop=False)
            for t in range(TT):
                o = b[:, t * L:(t + 1) * L]
                pe.matmul(o, K[n % 3][r, m, t * P:(t + 1) * P], Q[n % 3][r, m, :], start=False, stop=False)
                i = pe.matmul(o, sel[r, h, :], mT[n % 2][r, :], start=False, stop=(t == TT - 1))
            pe_s2.did(i)

        def exponentials(g):
            need(act, pe_s2, g + 1)
            need(act, pe_pv, max(g - 2, 0))
            act_exp.did(act.activation(prob[g % 3][:].rearrange("p t l -> p (t l)"), s2_bank[g % 2][:], ACT.Exp,
                                       scale=SCALE))

        def weighted(g):
            n, h, _, _ = head(g)
            j = h % OQ
            r = slice(j * OS, (j + 1) * OS)
            need(pe, act_exp, g + 1)
            if j == 0:
                need(pe, dve_ot)
            for t in range(TT):
                i = pe.matmul(pv_bank[r, 0:L], V[n % 3][:, t, h, :], prob[g % 3][:, t, :], start=(t == 0),
                              stop=(t == TT - 1))
            pe_pv.did(i)

        def copy_out(g):
            n, h, _, _ = head(g)
            need(dve, pe_pv, g + 1)
            need(dve, pe_misc)
            dve_ot.did(dve.tensor_copy(OT[h // OQ][:], pv_bank[:, 0:L]))

        def divide(n, t):
            need(pe, dve_ot)
            b = yield from claim()
            for q in range(H // OQ):
                i = pe.transpose(bank[b][:, q * P:(q + 1) * P], OT[q][:, t * P:(t + 1) * P], ident[:])
            pe_misc.did(i)
            yield
            need(dve, pe_misc)
            v = bank[b][:].rearrange("p (h c) -> p h c", c=OS)
            need(dve, dve_misc)
            dve_misc.did(dve.reciprocal(rden[:], v[:, :, D]))
            need(dve, dve_misc)
            dve_misc.did(dve.tensor_tensor(ao[:, t].rearrange("p (h d) -> p h d", d=D), v[:, :, 0:D],
                                           rden[:].rearrange("p (h o) -> p h o", o=1).to_broadcast([P, H, D]),
                                           ALU.mult))
            give(b)

        def output(n):
            b = yield from claim()
            for stage, count in turned["a", n]:
                need(pe, stage, count)
            for t in range(TT):
                i = product(bank[b][:, t * E:(t + 1) * E],
                            [lambda kc, t=t, q=q: aT[q][:, kc, t * P:(t + 1) * P] for q in range(2)],
                            [lambda kc, q=q: WoT[q][:, kc, :] for q in range(2)])
            pe_misc.did(i)
            yield
            need(dve, pe_misc)
            need(dve, pool_x2)
            v = x2[:, n * TT:(n + 1) * TT]
            dve_misc.did(dve.tensor_tensor(v, bank[b][:].rearrange("p (t e) -> p t e", t=TT), v, ALU.add))
            give(b)
            yield
            need(dve, dve_misc)
            need(dve, st_list)
            yield from norm(n, 1, v, x2n[n % 2])

        def route(n):
            b = yield from claim()
            for stage, count in turned["y", n]:
                need(pe, stage, count)
            for t in range(TT):
                terms = [(kc, a, w) for kc in range(KC) for a in yT for w in WgT]
                for k, (kc, a, w) in enumerate(terms):
                    i = pe.matmul(bank[b][:, t * NE:(t + 1) * NE], a[:, kc, t * P:(t + 1) * P], w[:, kc, :],
                                  start=(k == 0), stop=(k == len(terms) - 1))
            pe_misc.did(i)
            yield
            need(dve, pe_misc)
            dve_misc.did(dve.tensor_copy(lg[:], bank[b][:, 0:TT * NE].rearrange("p (t e) -> p t e", e=NE)))
            give(b)
            need(dve, dve_misc)
            dve_gate.did(dve.tensor_reduce(mx[:], lg[:], AX.X, ALU.max))

            def over(v):
                return v.rearrange("p (t o) -> p t o", o=1).to_broadcast([P, TT, NE])

            need(dve, dve_gate)
            dve_gate.did(dve.tensor_tensor(lg[:], lg[:], over(mx[:]), ALU.subtract))
            need(act, dve_gate)
            act_gate.did(act.activation(lg[:], lg[:], ACT.Exp))
            yield
            need(dve, act_gate)
            dve_gate.did(dve.tensor_reduce(sm[:], lg[:], AX.X, ALU.add))
            need(dve, dve_gate)
            dve_gate.did(dve.reciprocal(sm[:], sm[:]))
            need(dve, dve_gate)
            dve_gate.did(dve.tensor_tensor(lg[:], lg[:], over(sm[:]), ALU.mult))
            yield
            need(dve, dve_gate)
            shape = [P, TT, NE, NE]
            gj = lg[:].rearrange("p t (o e) -> p t o e", o=1).to_broadcast(shape)
            gi = lg[:].rearrange("p t (e o) -> p t e o", o=1).to_broadcast(shape)
            dve_gate.did(dve.tensor_tensor(larger[:], gj, gi, ALU.is_gt))
            dve_gate.did(dve.tensor_tensor(equal[:], gj, gi, ALU.is_equal))
            need(dve, dve_gate)
            dve_gate.did(dve.tensor_tensor(equal[:], equal[:], less[:].rearrange("p (o e) j -> p o e j", o=1)
                                           .to_broadcast(shape), ALU.mult))
            need(dve, dve_gate)
            dve_gate.did(dve.tensor_tensor(larger[:], larger[:], equal[:], ALU.add))
            need(dve, dve_gate)
            dve_gate.did(dve.tensor_reduce(rank[:], larger[:], AX.X, ALU.add))
            need(dve, dve_gate)
            T = slice(n * TT, (n + 1) * TT)
            dve_gate.did(dve.tensor_scalar(chosen[:, T], rank[:], float(TOP), None, ALU.is_lt))
            yield
            need(pe, dve_gate)
            b = yield from claim()
            for t in range(TT):
                terms = [(before, chosen[:, n * TT + t])] + [(onesb, chosen[:, n * TT + u]) for u in range(t)]
                terms.append((onesb, run[:]))
                for k, (m, c) in enumerate(terms):
                    i = pe.matmul(bank[b][:, t * NE:(t + 1) * NE], m[:], c, start=(k == 0), stop=(k == len(terms) - 1))
            pe_misc.did(i)
            need(dve, dve_gate)
            dve_gate.did(dve.tensor_tensor(weight[:, T], chosen[:, T], lg[:], ALU.mult))
            yield
            need(dve, pe_misc)
            dve_misc.did(dve.tensor_tensor(place[:, T], bank[b][:, 0:TT * NE].rearrange("p (t e) -> p t e", e=NE),
                                           base[:].rearrange("p (o e) -> p o e", o=1).to_broadcast([P, TT, NE]),
                                           ALU.add))
            give(b)
            for t in range(TT):
                need(dve, dve_gate)
                dve_gate.did(dve.tensor_tensor(run[:], run[:], chosen[:, n * TT + t], ALU.add))
            yield
            need(dve, dve_misc)
            dve_gate.did(dve.scalar_tensor_tensor(off[:], chosen[:, T], -FAR, place[:, T], ALU.mult, ALU.add))
            need(dve, dve_gate)
            dve_gate.did(dve.tensor_reduce(ends[:, 0], off[:], AX.X, ALU.min))
            need(dve, dve_gate)
            dve_gate.did(dve.tensor_tensor(off[:], chosen[:, T], place[:, T], ALU.mult))
            need(dve, dve_gate)
            dve_gate.did(dve.tensor_reduce(ends[:, 1], off[:], AX.X, ALU.max))
            need(dve, dve_gate)
            need(dve, st_list)
            dve_gate.did(dve.tensor_scalar(rows[n % 2][:, 0], ends[:, 0], FAR, None, ALU.add))
            dve_gate.did(dve.tensor_copy(rows[n % 2][:, 1], ends[:, 1]))
            yield
            need(pool, dve_gate)
            need(pool, dve_ln)
            need(pool, st_zero)
            for t in range(TT):
                for k in range(TOP):
                    st_list.did(pool.indirect_dma_start(
                        out=lists, out_offset=bass.IndirectOffsetOnAxis(ap=rows[n % 2][:, k, t:t + 1], axis=0),
                        in_=x2n[n % 2][:, t], in_offset=None))

        LAG2, LAGV = 18, 19
        starts = {}

        def at(g, piece):
            starts.setdefault(g, []).append(piece)

        for n in range(NB):
            g0 = (n - 1) * H
            if n >= 2:
                at(g0 - 6, lambda n=n: iter([load(n)]))
            at(g0 + 0, lambda n=n: norm1(n))
            at(g0 + 1, lambda n=n: turn_rows(("c", n), cin[n % 2], cT, ld_c[n % 2]))
            at(g0 + 2, lambda n=n: masks(n))
            for k, g in enumerate((3, 5, 6, 7)):
                at(g0 + g, lambda n=n, k=k: project(n, WkT, cT, 2 * k, K, neglo_k, 0))
            at(g0 + 5, lambda n=n: turn_rows(("x", n), xn, xT, dve_ln))
            for k, g in enumerate((9, 10, 11, 13)):
                at(g0 + g, lambda n=n, k=k: project(n, WqT, xT, 2 * k, Q, neglo_q, 1))
            at(g0 + 14, lambda n=n: values(n))
            at((n + 1) * H, lambda n=n: max_rows(n))
            g1 = n * H + H - 1 + LAGV + 1
            at(g1 + 0, lambda n=n: divide(n, 0))
            at(g1 + 1, lambda n=n: divide(n, 1))
            at(g1 + 3, lambda n=n: turn_rows(("a", n), ao, aT, dve_misc))
            at(g1 + 5, lambda n=n: output(n))
            at(g1 + 11, lambda n=n: turn_rows(("y", n), x2n[n % 2], yT, dve_ln))
            at(g1 + 13, lambda n=n: route(n))

        NG = NB * H
        going = []
        for g in range(-H, max(starts) + 16):
            if 0 <= g < NG:
                scores_for_max(g)
            if 0 <= g - LAG2 < NG:
                scores(g - LAG2)
            if 0 <= g - LAGV < NG:
                weighted(g - LAGV)
            if 0 <= g < NG:
                take_max(g)
            if 0 <= g - LAG2 < NG:
                exponentials(g - LAG2)
            if 0 <= g - LAGV < NG and (g - LAGV) % OQ == OQ - 1:
                copy_out(g - LAGV)
            going = [p for p in going if next(p, "end") != "end"]
            for piece in starts.get(g, []):
                p = piece()
                if next(p, "end") != "end":
                    going.append(p)
        assert not going

        A.close()
        for engine in (sp, act, dve, pe, pool):
            for stage in (pe_misc, dve_misc, act_misc, pe_pv, pe_s2, act_exp, dve_ln, dve_gate, dve_ot, pool_ln,
                          pool_x2):
                need(engine, stage)

        w1_in.append(sb(top, "w1_in1", [P, KC, F]))
        w2_in.append(sb(top, "w2_in1", [P, MF, E]))
        W1p = [[sb(top, f"W1p{i}{q}", [P, KC, F], F32R) for q in range(2)] for i in range(2)]
        W2p = [[sb(top, f"W2p{i}{q}", [P, MF, E], F32R) for q in range(2)] for i in range(2)]
        b2_in = [sb(top, f"b2_in{i}", [P, E]) for i in range(3)]
        b1c = [sb(top, f"b1c{i}", [P, MF]) for i in range(2)]
        xg = [sb(top, f"xg{i}", [P, TS // P, E]) for i in range(2)]
        xgT = [[sb(top, f"xgT{i}{q}", [P, KC, TS], F32R) for q in range(2)] for i in range(2)]
        hf = [sb(top, f"hf{i}", [P, 2, TS]) for i in range(2)]
        hp = [[sb(top, f"hp{i}{q}", [P, MF, TS], F32R) for q in range(2)] for i in range(2)]
        y = [sb(top, f"y{i}", [P, TS // P, E]) for i in range(2)]
        x_bank = [top.enter_context(nc.psum_tensor("x_bank", [P, 512], F32))]
        h_bank = [top.enter_context(nc.psum_tensor(f"h_bank{i}", [P, 2, TS], F32)) for i in range(4)]
        y_bank = [top.enter_context(nc.psum_tensor(f"y_bank{i}", [P, TS // P, E], F32)) for i in range(2)]
        n_bank = top.enter_context(nc.psum_tensor("n_bank", [P, NE], F32))

        count = sb(top, "count", [P, NE])
        steps = sb(top, "steps", [P, NE, MORE])
        extra = sb(top, "extra", [P, NE])
        prod = sb(top, "prod", [P, NE, NE])
        pre = sb(top, "pre", [P, NE])
        upto = sb(top, "upto", [P, NE])
        last = sb(top, "last", [P, 1])
        number = sb(top, "number", [P, EXTRA])
        over_ = sb(top, "over_", [P, EXTRA, NE])
        past = sb(top, "past", [P, EXTRA, NE])
        tile_e = sb(top, "tile_e", [P, EXTRA])
        tile_s = sb(top, "tile_s", [P, EXTRA])
        table = sb(top, "table", [P, 2, EXTRA], I32)
        zrow = sb(top, "zrow", [P, NE], I32)
        place_ = sb(top, "place_", [P, NT, NE])
        beyond = sb(top, "beyond", [P, NT, NE])
        shift = sb(top, "shift", [P, 2, NE])
        low = sb(top, "low", [P, NT])
        is_k = sb(top, "is_k", [P, 2, NT, NE])
        picked = sb(top, "picked", [P, NT, NE])
        found = sb(top, "found", [P, 2, NT])
        gates = sb(top, "gates", [P, 2, NT])
        index = sb(top, "index", [P, 2, NT], I32)

        dve_r, pool_r, pe_r = step("dve_r"), step("pool_r"), step("pe_r")
        ld_xg = [step(f"ld_xg{i}", 16) for i in range(2)]
        ld_b2 = [step(f"ld_b2{i}", 16) for i in range(3)]
        act_w, dve_w1, dve_w2 = step("act_w"), step("dve_w1"), step("dve_w2")
        pe_xg, act_xg, dve_xg = step("pe_xg"), step("act_xg"), step("dve_xg")
        pe_h, act_h, dve_h = step("pe_h"), step("act_h"), step("dve_h")
        pe_y, dve_y = step("pe_y"), step("dve_y")
        dve_b1 = step("dve_b1")
        st_y = step("st_y", 16)
        ld_r = [step(f"ld_r{i}", 16) for i in range(4)]
        dve_o = step("dve_o")
        st_out = step("st_out", 16)

        for k in range(MORE):
            pool_r.did(pool.memset(steps[:, :, k:k + 1], float(TS * (k + 1))))
        for k in range(EXTRA):
            pool_r.did(pool.memset(number[:, k:k + 1], float(k)))

        def tables():
            def chain(ins):
                dve_r.did(ins)
                need(dve, dve_r)

            def row(v, shape):
                return v.rearrange("p (o e) -> p o e", o=1).to_broadcast(shape)

            def col(v, shape):
                return v.rearrange("p (e o) -> p e o", o=1).to_broadcast(shape)

            pe_r.did(pe.matmul(n_bank[:], onesb[:], run[:], start=True, stop=True))
            need(dve, pe_r)
            need(dve, pool_r)
            chain(dve.tensor_copy(count[:], n_bank[:]))
            chain(dve.tensor_tensor(zrow[:], count[:], base[:], ALU.add))
            chain(dve.tensor_tensor(steps[:], col(count[:], [P, NE, MORE]), steps[:], ALU.is_gt))
            chain(dve.tensor_reduce(extra[:], steps[:], AX.X, ALU.add))
            chain(dve.tensor_tensor(prod[:], row(extra[:], [P, NE, NE]), less[:], ALU.mult))
            chain(dve.tensor_reduce(pre[:], prod[:], AX.X, ALU.add))
            chain(dve.tensor_tensor(upto[:], pre[:], extra[:], ALU.add))
            chain(dve.tensor_scalar(last[:], upto[:, NE - 1:NE], -1.0, None, ALU.add))
            chain(dve.tensor_scalar(number[:], number[:], last[:], None, ALU.min))
            full = [P, EXTRA, NE]
            chain(dve.tensor_tensor(over_[:], row(upto[:], full), col(number[:], full), ALU.is_le))
            chain(dve.tensor_reduce(tile_e[:], over_[:], AX.X, ALU.add))
            chain(dve.tensor_tensor(past[:], over_[:], row(extra[:], full), ALU.mult))
            chain(dve.tensor_reduce(tile_s[:], past[:], AX.X, ALU.add))
            chain(dve.tensor_tensor(tile_s[:], number[:], tile_s[:], ALU.subtract))
            chain(dve.tensor_scalar(tile_s[:], tile_s[:], 1.0, float(TS), ALU.add, ALU.mult))
            chain(dve.scalar_tensor_tensor(table[:, 0], tile_e[:], float(REGION), tile_s[:], ALU.mult, ALU.add))
            chain(dve.tensor_copy(table[:, 1], tile_e[:]))
            done = dve_r.count

            bt = base[:].rearrange("p (o e) -> p o e", o=1).to_broadcast([P, NT, NE])
            chain(dve.tensor_tensor(place_[:], place[:], bt, ALU.subtract))
            chain(dve.tensor_scalar(shift[:, 0], base[:], TS / REGION, None, ALU.mult))
            chain(dve.tensor_scalar(shift[:, 1], pre[:], float(TS), float((NE - 1) * TS), ALU.mult, ALU.add))
            chain(dve.tensor_tensor(shift[:, 1], shift[:, 1], shift[:, 0], ALU.subtract))
            chain(dve.tensor_scalar(beyond[:], place_[:], float(TS), None, ALU.is_ge))
            wide = [P, NT, NE]
            chain(dve.tensor_tensor(beyond[:], beyond[:], row(shift[:, 1], wide), ALU.mult))
            chain(dve.tensor_tensor(place_[:], place_[:], row(shift[:, 0], wide), ALU.add))
            chain(dve.tensor_tensor(place_[:], place_[:], beyond[:], ALU.add))
            chain(dve.scalar_tensor_tensor(beyond[:], chosen[:], -FAR, place[:], ALU.mult, ALU.add))
            chain(dve.tensor_reduce(low[:], beyond[:], AX.X, ALU.min))
            chain(dve.tensor_tensor(is_k[:, 0], beyond[:], col(low[:], wide), ALU.is_equal))
            chain(dve.tensor_tensor(is_k[:, 1], chosen[:], is_k[:, 0], ALU.subtract))
            for k in range(TOP):
                chain(dve.tensor_tensor(picked[:], is_k[:, k], place_[:], ALU.mult))
                chain(dve.tensor_reduce(found[:, k], picked[:], AX.X, ALU.add))
                chain(dve.tensor_copy(index[:, k], found[:, k]))
                chain(dve.tensor_tensor(picked[:], is_k[:, k], weight[:], ALU.mult))
                chain(dve.tensor_reduce(gates[:, k], picked[:], AX.X, ALU.add))
            return done

        W1_d = W1.rearrange("e (k p) f -> e p k f", p=P)
        W2_d = W2.rearrange("e (m p) d -> e p m d", p=P)
        b2_d = b2.rearrange("(o e) d -> o e d", o=1)

        def load_tile(i):
            k = i % 2
            if i < NE:
                r, e = i * REGION, i
                rows_, w1, w2, bb = lists[r:r + TS, :], W1_d[e], W2_d[e], b2_d[:, e, :]
                if i == 0:
                    need(sp, st_list)
                    need(sp, st_zero)
            else:
                if i == NE:
                    need(sp, dve_r, table_done)
                    need(sp, ld_xg[0])
                    need(sp, ld_xg[1])
                    for e in range(NE):
                        z = sp.value_load(zrow[0:1, e:e + 1], min_val=e * REGION, max_val=e * REGION + REGION - TS)
                        st_zero.did(sp.dma_start(lists[bass.ds(z, TS), :].rearrange("(t p) e -> p t e", p=P), zero[:]))
                    need(sp, st_zero)
                j = i - NE
                r = sp.value_load(table[0:1, 0, j:j + 1], min_val=0, max_val=NE * REGION - TS)
                e = sp.value_load(table[0:1, 1, j:j + 1], min_val=0, max_val=NE - 1)
                rows_ = lists[bass.ds(r, TS), :]
                w1, w2 = (w[bass.ds(e, 1)].rearrange("o p a b -> (o p) a b") for w in (W1_d, W2_d))
                bb = b2_d[:, bass.ds(e, 1), :].rearrange("o u d -> o (u d)")
            need(sp, pe_xg)
            ld_xg[k].did(sp.dma_start(xg[k][:], rows_.rearrange("(t p) e -> p t e", p=P)))
            if i:
                need(sp, dve_w1)
                ld_w1[k].did(sp.dma_start(w1_in[k][:], w1))
                need(sp, dve_w2)
                ld_w2[k].did(sp.dma_start(w2_in[k][:], w2))
            need(sp, dve_y)
            ld_b2[i % 3].did(sp.dma_start(b2_in[i % 3][:], bb.to_broadcast([P, E])))

        def split(i, which, part):
            src, dst, ld, stage, reader = ((w1_in, W1p, ld_w1, dve_w1, pe_h), (w2_in, W2p, ld_w2, dve_w2, pe_y))[which]
            k = i % 2
            n = src[k].shape[1] // 2
            c = slice(part * n, (part + 1) * n)
            need(act, ld[k])
            need(act, reader)
            act_w.did(act.activation(dst[k][0][:, c], src[k][:, c], ACT.Copy))
            yield
            need(dve, ld[k])
            need(dve, reader)
            need(dve, act_w)
            stage.did(dve.tensor_tensor(dst[k][1][:, c], src[k][:, c], dst[k][0][:, c].bitcast(F32), ALU.subtract))

        def turn_tile(i):
            k = i % 2
            need(pe, ld_xg[k])
            need(pe, dve_xg)
            for kc in range(KC):
                for t in range(TS // P):
                    ins = pe.transpose(x_bank[0][:, kc * TS + t * P:kc * TS + (t + 1) * P],
                                       xg[k][:, t, kc * P:(kc + 1) * P], ident[:])
            pe_xg.did(ins)
            need(act, pe_xg)
            need(act, pe_h)
            v = x_bank[0][:].rearrange("p (k l) -> p k l", k=KC)
            act_xg.did(act.activation(xgT[k][0][:], v, ACT.Copy))
            need(dve, act_xg)
            dve_xg.did(dve.tensor_tensor(xgT[k][1][:], v, xgT[k][0][:].bitcast(F32), ALU.subtract))

        def bias1(i):
            if i < NE:
                return b1T[:, i * MF:(i + 1) * MF]
            e = dve.value_load(table[0:1, 1, i - NE:i - NE + 1], min_val=0, max_val=NE - 1)
            need(dve, act_h)
            dve_b1.did(dve.tensor_copy(b1c[i % 2][:], b1T[:, bass.ds(e * MF, MF)]))
            return b1c[i % 2][:]

        def hidden(i, pair):
            k = i % 2
            b = h_bank[pair]
            need(pe, act_h, max(act_h.count - 6, 0))
            if pair == 0:
                need(pe, dve_w1)
                need(pe, dve_xg)
            for u in range(2):
                m = 2 * pair + u
                terms = [(kc, a, c) for kc in range(KC) for a, c in ((0, 0), (0, 1), (1, 0))]
                for j, (kc, a, c) in enumerate(terms):
                    ins = pe.matmul(b[:, u, :], W1p[k][a][:, kc, m * P:(m + 1) * P], xgT[k][c][:, kc, :],
                                    start=(j == 0), stop=(j == len(terms) - 1))
            pe_h.did(ins)

        def gelu(i, pair, bias):
            need(act, pe_h, i * (MF // 2) + pair + 1)
            need(act, dve_h, max(dve_h.count - 2, 0))
            need(act, dve_b1)
            for u in range(2):
                m = 2 * pair + u
                act_h.did(act.activation(hf[pair % 2][:, u], h_bank[pair][:, u], ACT.Gelu, bias=bias[:, m:m + 1]))

        def hidden_parts(i, pair):
            k = i % 2
            c = slice(2 * pair, 2 * pair + 2)
            need(dve, act_h)
            need(dve, pe_y)
            dve_h.did(dve.tensor_copy(hp[k][0][:, c], hf[pair % 2][:]))
            need(dve, dve_h)
            dve_h.did(dve.tensor_tensor(hp[k][1][:, c], hf[pair % 2][:], hp[k][0][:, c].bitcast(F32), ALU.subtract))

        def outputs(i, t):
            k = i % 2
            need(pe, dve_h, h_done[i])
            need(pe, dve_w2)
            need(pe, dve_y)
            terms = [(m, a, c) for m in range(MF) for a, c in ((0, 0), (0, 1), (1, 0))]
            for j, (m, a, c) in enumerate(terms):
                ins = pe.matmul(y_bank[k][:, t, :], hp[k][a][:, m, t * P:(t + 1) * P], W2p[k][c][:, m, :],
                                start=(j == 0), stop=(j == len(terms) - 1))
            if t == TS // P - 1:
                pe_y.did(ins)

        def store(i):
            k = i % 2
            need(dve, pe_y, i + 1)
            need(dve, ld_b2[i % 3])
            need(dve, st_y)
            for t in range(TS // P):
                dve_y.did(dve.tensor_tensor(y[k][:, t], y_bank[k][:, t], b2_in[i % 3][:], ALU.add))
            need(act, dve_y)
            st_y.did(act.dma_start(results[i * TS:(i + 1) * TS, :].rearrange("(t p) e -> p t e", p=P), y[k][:]))

        h_done = {}
        table_done = None
        load_tile(0)
        load_tile(1)
        for which in range(2):
            for part in range(2):
                if which == 0:
                    for _ in split(0, which, part):
                        pass
        turn_tile(0)
        table_done = tables()
        for i in range(NTILE + 1):
            if i < NTILE:
                bias = bias1(i)
                for pair in range(MF // 2):
                    hidden(i, pair)
                    gelu(i, pair, bias)
                    which, j = (1, i) if pair < 2 else (0, i + 1)
                    s = split(j, which, pair % 2) if j < NTILE else iter(())
                    next(s, None)
                    hidden_parts(i, pair)
                    next(s, None)
                h_done[i] = dve_h.count
            if i + 1 < NTILE:
                turn_tile(i + 1)
            if i:
                for t in range(TS // P):
                    outputs(i - 1, t)
                store(i - 1)
            if i + 2 < NTILE:
                load_tile(i + 2)

        got = [[sb(top, f"got{k}{j}", [P, E]) for j in range(4)] for k in range(TOP)]
        need(pool, st_y)
        need(pool, dve_r)

        def gather(T):
            need(pool, dve_o)
            for k in range(TOP):
                ld_r[T % 4].did(pool.indirect_dma_start(
                    out=got[k][T % 4][:], out_offset=None, in_=results,
                    in_offset=bass.IndirectOffsetOnAxis(ap=index[:, k, T:T + 1], axis=0)))

        for T in range(3):
            gather(T)
        for T in range(NT):
            if T + 3 < NT:
                gather(T + 3)
            need(dve, ld_r[T % 4])
            for k in range(TOP):
                need(dve, dve_o)
                dve_o.did(dve.scalar_tensor_tensor(x2[:, T], got[k][T % 4][:], gates[:, k, T:T + 1], x2[:, T],
                                                   ALU.mult, ALU.add))
            if T % 4 == 3:
                need(sp, dve_o)
                st_out.did(sp.dma_start(out_d[:, T - 3:T + 1], x2[:, T - 3:T + 1]))
        need(sp, st_out)


def kernel(x, ctx_1024, mask_BxS2_bf1, mask_BxSxS2_bf1, L0_xattn_Wq, L0_xattn_Wk, L0_xattn_Wv, L0_xattn_Wo,
           L0_xattn_bo, L0_ffn_w_gate, L0_ffn_W1, L0_ffn_b1, L0_ffn_W2, L0_ffn_b2):
    import concourse.bacc as bacc
    from concourse.bass_utils import run_bass_kernel_spmd

    named = dict(x=x, ctx_in=ctx_1024, pad=mask_BxS2_bf1, mask=mask_BxSxS2_bf1, Wq=L0_xattn_Wq, Wk=L0_xattn_Wk,
                 Wv=L0_xattn_Wv, Wo=L0_xattn_Wo, bo=L0_xattn_bo, w_gate=L0_ffn_w_gate, W1=L0_ffn_W1, b1=L0_ffn_b1,
                 W2=L0_ffn_W2, b2=L0_ffn_b2)
    nc = bacc.Bacc("TRN2", target_bir_lowering=False, num_devices=1)
    arrays, args = {}, {}
    for name, a in named.items():
        a = np.ascontiguousarray(a)
        if a.dtype == bool:
            a = a.view(np.uint8)
        arrays[f"in_{name}"] = a
        args[name] = nc.dram_tensor(f"in_{name}", a.shape, mybir.dt.from_np(a.dtype), kind="ExternalInput").ap()
    out = nc.dram_tensor("out_0", np.shape(x), F32, kind="ExternalOutput").ap()
    build(nc, out=out, **args)
    r = run_bass_kernel_spmd(nc, [arrays], core_ids=[0])
    return r.results[0]["out_0"]
```

```python
from contextlib import ExitStack

import numpy as np
import concourse.bass as bass
from concourse import mybir

F32 = mybir.dt.float32
F32R = mybir.dt.float32r
BF16 = mybir.dt.bfloat16
U8 = mybir.dt.uint8
I32 = mybir.dt.int32
I16 = mybir.dt.int16
ALU = mybir.AluOpType
ACT = mybir.ActivationFunctionType
AX = mybir.AxisListType

P = 128
LN_EPS = 1e-5
BIG = 2.0 ** 100
FAR = 2.0 ** 17


class Step:

    def __init__(self, ctx, nc, name, by=1):
        self.sem, self.by, self.count, self.waited = ctx.enter_context(nc.semaphore(name)), by, 0, {}

    def did(self, instruction):
        instruction.then_inc(self.sem, self.by)
        self.count += self.by


def need(engine, step, count=None):
    count = step.count if count is None else count
    if count > step.waited.get(engine, 0):
        engine.wait_ge(step.sem, count)
        step.waited[engine] = count


class Queue:

    def __init__(self, engine):
        self.engine, self.kept = engine, []

    def _keep(self, call, args, kwargs):
        entry = Entry(call, args, kwargs)
        self.kept.append(entry)
        return entry

    def matmul(self, *args, **kwargs):
        return self._keep(self.engine.matmul, args, kwargs)

    def transpose(self, *args, **kwargs):
        return self._keep(self.engine.transpose, args, kwargs)

    def wait_ge(self, *args):
        return self._keep(self.engine.wait_ge, args, {})

    def write(self, masked):
        for entry in self.kept:
            kwargs = dict(entry.kwargs)
            unmasked = kwargs.pop("unmasked", {})
            if not masked:
                if unmasked is None:
                    continue
                kwargs.update(unmasked)
            instruction = entry.call(*entry.args, **kwargs)
            for sem, by in entry.raised:
                instruction.then_inc(sem, by)


class Entry:
    def __init__(self, call, args, kwargs):
        self.call, self.args, self.kwargs, self.raised = call, args, kwargs, []

    def then_inc(self, sem, by):
        self.raised.append((sem, by))


def build(nc, x, ctxT, pad, pad_c_in, mask, maskT, WqT_in, WkT_in, WvT_in, WoT_in, bo, wgT_in, W1, b1T_in, W2, b2, out):
    pe, dve, act, pool, sp = nc.tensor, nc.vector, nc.scalar, nc.gpsimd, nc.sync
    NB, L, E = x.shape
    NE, _, F = W1.shape
    D = 16
    H = E // D
    TT = L // P
    KC = E // P
    NT = NB * TT
    HALF = 4 * D
    MQ = H * HALF // P
    MF = F // P
    OQ = 4
    OS = P // OQ
    SCALE = 1.0 / float(np.sqrt(D))
    TS = 256
    TOP = 2
    REGION = NT * P + TS
    EXTRA = (TOP * NT * P - NE) // TS
    NTILE = NE + EXTRA
    MORE = NT * P // TS - 1
    assert TT == 2 and KC == 2 and H == 16 and MQ == 8

    x_d = x.rearrange("n (t p) e -> n p t e", p=P)
    c_d = ctxT.rearrange("n (k p) l -> n p k l", p=P)
    m_d = mask.rearrange("n (t p) k -> n p t k", p=P)
    mT_d = maskT.rearrange("n (t p) q -> n p t q", p=P)
    out_d = out.rearrange("n (t p) e -> p (n t) e", p=P)
    W = E + 2
    NONE = 2.0 ** 20
    lists = nc.dram_tensor("lists", [NE * REGION, W], F32, kind="Internal").ap()
    results = nc.dram_tensor("results", [TOP * NT * P + 1, E], F32, kind="Internal").ap()

    top = ExitStack()
    with top:
        def step(name, by=1):
            return Step(top, nc, name, by)

        def sb(ctx, name, shape, dt=F32):
            return ctx.enter_context(nc.sbuf_tensor(name, shape, dt))

        ident = sb(top, "ident", [P, P])
        x2 = sb(top, "x2", [P, NT, E])
        b1T = sb(top, "b1T", [P, NE * MF])
        less = sb(top, "less", [P, NE, NE])
        base = sb(top, "base", [P, NE])
        place = sb(top, "place", [P, NT, NE])
        chosen = sb(top, "chosen", [P, NT, NE], BF16)
        weight = sb(top, "weight", [P, NT, NE])
        run = sb(top, "run", [P, NE], BF16)
        onesb = sb(top, "onesb", [P, P], BF16)
        zero = sb(top, "zero", [P, TS // P, W])
        ids = sb(top, "ids", [P, NT], I32)
        w1_in = [sb(top, "w1_in0", [P, KC, F])]
        w2_in = [sb(top, "w2_in0", [P, MF, E])]

        A = ExitStack()
        bank = [A.enter_context(nc.psum_tensor(f"bank{i}", [P, 512], F32)) for i in range(8)]
        s1_bank, s2_bank, pv_bank = bank[0:2], bank[2:4], bank[4]
        MISC = (5, 6, 7)

        WqT = [sb(A, f"WqT{i}", [P, KC, E], F32R) for i in range(2)]
        WkT = [sb(A, f"WkT{i}", [P, KC, E], F32R) for i in range(2)]
        WvT = [sb(A, f"WvT{i}", [P, KC, E], F32R) for i in range(2)]
        WoT = [sb(A, f"WoT{i}", [P, KC, E], F32R) for i in range(2)]
        WgT = sb(A, "WgT", [P, KC, NE])
        bo_b = sb(A, "bo_b", [P, E])
        padB = sb(A, "padB", [P, NT])
        padR = sb(A, "padR", [P, NB, L], BF16)
        identb = sb(A, "identb", [P, P], BF16)
        before = sb(A, "before", [P, P], BF16)
        pick_q = [sb(A, f"pick_q{i}", [P, P // D, 4, D], F32R) for i in range(2)]
        pick_k = [sb(A, f"pick_k{i}", [P, P // D, 4, D], F32R) for i in range(2)]
        sel = sb(A, "sel", [P, H, P], F32R)
        half = sb(A, "half", [P, TT])
        nbig = sb(A, "nbig", [P, 1])
        xin = [sb(A, f"xin{i}", [P, TT, E]) for i in range(2)]
        cin = [sb(A, f"cin{i}", [P, KC, L]) for i in range(2)]
        min_ = [sb(A, f"min{i}", [P, 2, TT, L], U8) for i in range(2)]
        stats = [sb(A, f"stats{i}", [P, TT, 6]) for i in range(2)]
        mv = [sb(A, f"mv{i}", [P, TT, 2]) for i in range(2)]
        ve = [sb(A, f"ve{i}", [P, TT]) for i in range(2)]
        rstd = [sb(A, f"rstd{i}", [P, TT]) for i in range(2)]
        free_ = sb(A, "free_", [P, TT])
        nanb = sb(A, "nanb", [P, NT])
        Bq = [sb(A, f"Bq{i}", [P, TT, L], BF16) for i in range(3)]
        Bk = [sb(A, f"Bk{i}", [P, TT, L], BF16) for i in range(3)]
        Q = [sb(A, f"Q{i}", [P, MQ, L], F32R) for i in range(3)]
        K = [sb(A, f"K{i}", [P, MQ, L], F32R) for i in range(3)]
        V = [sb(A, f"V{i}", [P, TT, H, OS]) for i in range(3)]

        any_mask = sb(A, "any_mask", [P, 1], I32)
        first = ExitStack()
        Wst = sb(first, "Wst", [P, 4, KC, E])
        pad_c = sb(first, "pad_c", [P, NT], U8)
        pad_r = sb(first, "pad_r", [P, NB, L], U8)
        masks_in = sb(first, "masks_in", [P, NB * L * L // P], U8)
        least = sb(first, "least", [P, 2])
        open_ = sb(first, "open_", [P, 1], BF16)
        rows16 = sb(first, "rows16", [P, D])
        rowsm = sb(first, "rowsm", [P, 1])

        ld_w = step("ld_w", 16)
        ld_x = [step(f"ld_x{i}", 16) for i in range(2)]
        ld_c = [step(f"ld_c{i}", 16) for i in range(2)]
        ld_m = [step(f"ld_m{i}", 16) for i in range(2)]
        ld_w1 = [step(f"ld_w1{i}", 16) for i in range(2)]
        ld_w2 = [step(f"ld_w2{i}", 16) for i in range(2)]
        st_list = [step(f"st_list{i}", 16) for i in range(2)]
        st_zero = step("st_zero", 16)
        ld_masks = step("ld_masks", 16)
        pe_flag, dve_flag = step("pe_flag"), step("dve_flag")
        pool_c = step("pool_c")
        dve_c = step("dve_c")
        pe_misc, act_misc, dve_misc = step("pe_misc"), step("act_misc"), step("dve_misc")
        act_bq, dve_bk, dve_lo = step("act_bq"), step("dve_bk"), step("dve_lo")
        pe_s1, dve_max = step("pe_s1"), step("dve_max")
        pe_s2, act_exp = step("pe_s2"), step("act_exp")
        pe_pv, dve_ot = step("pe_pv"), step("dve_ot")
        dve_ln, pool_ln, pool_x2 = step("dve_ln"), step("pool_ln"), step("pool_x2")
        dve_gate, act_gate = step("dve_gate"), step("act_gate")

        for i, w in enumerate((WkT_in, WqT_in, WvT_in, WoT_in)):
            ld_w.did(act.dma_start(Wst[:, i], w.rearrange("(k p) f -> p k f", p=P)))
        ld_w.did(act.dma_start(WgT[:], wgT_in.rearrange("(k p) e -> p k e", p=P)))
        ld_w.did(act.dma_start(b1T[:], b1T_in))
        ld_w.did(act.dma_start(bo_b[:], bo.rearrange("(o e) -> o e", o=1).to_broadcast([P, E])))
        ld_w.did(act.dma_start(pad_c[:], pad_c_in))
        ld_w.did(act.dma_start(pad_r[:].rearrange("p n l -> p (n l)"), pad.rearrange("(o n) l -> o (n l)", o=1)
                               .to_broadcast([P, NB * L])))

        made = {}

        def load(n):
            need(sp, dve_ln)
            need(sp, pool_ln)
            need(sp, pool_x2)
            need(sp, act_misc)
            need(sp, dve_lo)
            need(sp, act_bq)
            need(sp, dve_bk)
            ld_c[n % 2].did(sp.dma_start(cin[n % 2][:], c_d[n]))
            ld_x[n % 2].did(sp.dma_start(xin[n % 2][:], x_d[n]))
            ld_m[n % 2].did(sp.dma_start(min_[n % 2][:, 0], m_d[n]))
            ld_m[n % 2].did(sp.dma_start(min_[n % 2][:, 1], mT_d[n]))

        load(0)
        ld_masks.did(sp.dma_start(masks_in[:], mask.rearrange("n q k -> (n q k)").rearrange("(p f) -> p f", p=P)))
        load(1)

        pool_c.did(pool.memset(ident[:], 0.0))
        pool_c.did(pool.memset(half[:], -0.5))
        pool_c.did(pool.memset(nbig[:], -BIG))
        pool_c.did(pool.memset(less[:], 1.0))
        pool_c.did(pool.memset(before[:], 1.0))
        pool_c.did(pool.memset(onesb[:], 1.0))
        pool_c.did(pool.memset(run[:], 0.0))
        pool_c.did(pool.memset(zero[:, :, 0:E + 1], 0.0))
        pool_c.did(pool.memset(zero[:, :, E + 1:W], NONE))
        pool_c.did(pool.iota(ids[:], pattern=[[TOP * P, NT]], base=1, channel_multiplier=TOP))
        for e in range(NE):
            pool_c.did(pool.memset(base[:, e:e + 1], float(e * REGION)))
        need(pool, pool_c)
        pool_c.did(pool.affine_select(out=ident[:], in_=ident[:], compare_op=ALU.not_equal, fill=1.0, base=0,
                                      pattern=[[-1, P]], channel_multiplier=1))
        pool_c.did(pool.affine_select(out=less[:], in_=less[:], compare_op=ALU.is_gt, fill=0.0, base=0,
                                      pattern=[[1, NE], [-1, NE]], channel_multiplier=0))
        pool_c.did(pool.affine_select(out=before[:], in_=before[:], compare_op=ALU.is_gt, fill=0.0, base=0,
                                      pattern=[[1, P]], channel_multiplier=-1))
        for i in range(3):
            pool_c.did(pool.memset(V[i][:, :, :, D:], 0.0))
        need(pool, pool_c)
        for i in range(3):
            pool_c.did(pool.memset(V[i][:, :, :, D:D + 1], 1.0))
        need(sp, pool_c)
        for e in range(NE):
            st_zero.did(sp.dma_start(lists[e * REGION:e * REGION + TS, :].rearrange("(t p) e -> p t e", p=P), zero[:]))
        ld_w1[0].did(sp.dma_start(w1_in[0][:], W1[0].rearrange("(k p) f -> p k f", p=P)))
        ld_w2[0].did(sp.dma_start(w2_in[0][:], W2[0].rearrange("(m p) d -> p m d", p=P)))

        need(dve, pool_c)
        i4 = ident[:].rearrange("p (a c d) -> p a c d", c=4, d=D)
        dve_c.did(dve.tensor_reduce(rows16[:], ident[:].rearrange("p (a h) -> p h a", h=D), AX.X, ALU.add))
        dve_c.did(dve.tensor_reduce(rowsm[:], i4[:, :, 0:2, :].rearrange("p a c d -> p a (c d)"), AX.XY, ALU.add))
        dve_c.did(dve.tensor_copy(identb[:], ident[:]))
        need(dve, dve_c)
        dve_c.did(dve.tensor_scalar(sel[:], rows16[:].rearrange("p (h o) -> p h o", o=1).to_broadcast([P, H, P]),
                                    rowsm[:], None, ALU.mult))
        features = ident[:].rearrange("p (s o d) -> p s o d", o=1, d=D).to_broadcast([P, P // D, 2, D])
        for part in range(2):
            for other in range(2):
                for rows_ in (pick_q[part][:, :, other::2, :], pick_k[part][:, :, 2 * other:2 * other + 2, :]):
                    dve_c.did(dve.tensor_scalar(rows_, features, float(part == other), None, ALU.mult))
        need(dve, ld_masks)
        need(dve, ld_w)
        dve_flag.did(dve.tensor_reduce(least[:, 0:1], masks_in[:].bitcast(I16), AX.X, ALU.min))
        dve_flag.did(dve.tensor_reduce(least[:, 1:2], pad_c[:], AX.X, ALU.min))
        need(dve, dve_flag)
        dve_flag.did(dve.scalar_tensor_tensor(open_[:], least[:, 0:1], 257.0, least[:, 1:2], ALU.is_ge, ALU.mult))
        need(pe, dve_flag)
        need(pe, pool_c)
        pe_flag.did(pe.matmul(bank[MISC[0]][:, 0:1], onesb[:], open_[:], start=True, stop=True))
        need(dve, pe_flag)
        dve_flag.did(dve.tensor_scalar(any_mask[:], bank[MISC[0]][:, 0:1], float(P), None, ALU.is_lt))
        need(pe, dve_flag)
        hidden_keys = pe.value_load(any_mask[0:1, 0:1], min_val=0, max_val=1)
        pe = Queue(nc.tensor)

        readers = {b: () for b in MISC}
        turns, given = list(MISC), []

        def take():
            if not turns:
                turns.append(given.pop(0))
            b = turns.pop(0)
            for stage, count in readers[b]:
                need(pe, stage, count)
            return b

        def claim():
            while not turns:
                yield
            return take()

        def give(b):
            readers[b] = ((act_misc, act_misc.count), (dve_misc, dve_misc.count))
            given.append(b)

        def parts(src, hi, lo):
            act_misc.did(act.activation(hi, src, ACT.Copy))
            need(dve, act_misc)
            dve_misc.did(dve.tensor_tensor(lo, src, hi.bitcast(F32), ALU.subtract))

        need(act, ld_w)
        need(dve, ld_w)
        need(pe, pool_c)
        need(pe, dve_c)
        for i, w in enumerate((WkT, WqT, WvT, WoT)):
            parts(Wst[:, i], w[0][:], w[1][:])
        need(pe, act_misc)
        need(pe, dve_misc)
        dve_misc.did(dve.tensor_scalar(padB[:], pad_c[:], BIG, None, ALU.mult))
        dve_misc.did(dve.tensor_scalar(padR[:], pad_r[:], BIG, -2.0 * BIG, ALU.mult, ALU.add))
        weights_done = dve_misc.count
        first.close()
        for engine in (act, dve, pool):
            need(engine, pe_misc)
            need(engine, dve_misc)
            need(engine, dve_c)
        xn = sb(A, "xn", [P, TT, E])
        xT = [sb(A, f"xT{i}", [P, KC, L], F32R) for i in range(2)]
        cT = [sb(A, f"cT{i}", [P, KC, L], F32R) for i in range(2)]
        flat = [[sb(A, f"flat{w}{i}", [P, KC, L], F32R) for i in range(2)] for w in range(2)]
        nmax = [sb(A, f"nmax{i}", [P, H, TT]) for i in range(2)]
        mrep = sb(A, "mrep", [P, TT, 2, 4, H])
        mT = [sb(A, f"mT{i}", [P, L], F32R) for i in range(2)]
        prob = [sb(A, f"prob{i}", [P, TT, L]) for i in range(3)]
        OT = [[sb(A, f"OT{i}{q}", [P, L]) for q in range(H // OQ)] for i in range(2)]
        rden = sb(A, "rden", [P, H])
        ao = sb(A, "ao", [P, TT, E])
        aT = [sb(A, f"aT{i}", [P, KC, L], F32R) for i in range(2)]
        x2n = [sb(A, f"x2n{i}", [P, TT, W]) for i in range(2)]
        yT = sb(A, "yT", [P, KC, L])
        lg = sb(A, "lg", [P, TT, NE])
        mx = sb(A, "mx", [P, TT])
        sm = sb(A, "sm", [P, TT])
        gate = sb(A, "gate", [P, TT, NE])
        larger = sb(A, "larger", [P, TT, NE, NE])
        equal = sb(A, "equal", [P, TT, NE, NE])
        rank = sb(A, "rank", [P, TT, NE])
        off = sb(A, "off", [P, TT, NE])
        ends = sb(A, "ends", [P, 2, TT])
        rows = [sb(A, f"rows{i}", [P, 2, TT], I32) for i in range(2)]
        pool_c.did(pool.memset(mrep[:], 0.0))

        def wait_made(tag):
            while tag not in made:
                yield
            for stage, count in made[tag]:
                need(pe, stage, count)

        read = {}

        def turn_rows(source, src, tag, dst):
            while source not in made:
                yield
            b = yield from claim()
            yield from wait_made(source)
            for kc in range(KC):
                for t in range(TT):
                    i = pe.transpose(bank[b][:, kc * L + t * P:kc * L + t * P + P], src[:, t, kc * P:(kc + 1) * P],
                                     ident[:])
            pe_misc.did(i)
            here = read[source] = pe_misc.count
            yield
            need(act, pe_misc, here)
            need(dve, pe_misc, here)
            v = bank[b][:].rearrange("p (k l) -> p k l", k=KC)
            if len(dst) == 2:
                parts(v, dst[0][:], dst[1][:])
            else:
                act_misc.did(act.activation(dst[0][:], v, ACT.Copy))
            give(b)
            here = ((act_misc, act_misc.count), (dve_misc, dve_misc.count))
            yield
            made[tag] = here

        def split_ctx(n):
            need(act, ld_c[n % 2])
            need(act, pe_misc, read.get(("c", n - 1), 0))
            act_misc.did(act.activation(cT[0][:], cin[n % 2][:], ACT.Copy))
            need(dve, ld_c[n % 2])
            need(dve, act_misc)
            dve_lo.did(dve.tensor_tensor(cT[1][:], cin[n % 2][:], cT[0][:].bitcast(F32), ALU.subtract))
            here = ((act_misc, act_misc.count), (dve_lo, dve_lo.count))
            yield
            made["c", n] = here

        def product(o, lhs, rhs):
            terms = [(lhs[a], rhs[c], kc) for kc in range(KC) for a, c in ((0, 0), (0, 1), (1, 0))]
            for j, (l, r, kc) in enumerate(terms):
                i = pe.matmul(o, l(kc), r(kc), start=(j == 0), stop=(j == len(terms) - 1))
            return i

        def norm(n, which, src, dst, last_read):
            need(dve, pool_ln)
            for t in range(TT):
                dve_ln.did(dve.bn_stats(stats[which][:, t], src[:, t]))
            yield
            need(dve, dve_ln)
            for t in range(TT):
                dve_ln.did(dve.bn_aggr(mv[which][:, t], stats[which][:, t]))
            need(pool, dve_ln)
            pool_ln.did(pool.tensor_scalar(ve[which][:], mv[which][:, :, 1], LN_EPS, None, ALU.add))
            need(pool, pool_ln)
            pool_ln.did(pool.tensor_tensor(rstd[which][:], ve[which][:], half[:], ALU.pow))
            here = pool_ln.count
            yield
            yield
            need(dve, pool_ln, here)
            need(dve, pe_misc, read.get(last_read, 0))
            for t in range(TT):
                dve_ln.did(dve.tensor_scalar(dst[:, t, 0:E], src[:, t], mv[which][:, t, 0:1], rstd[which][:, t:t + 1],
                                             ALU.subtract, ALU.mult))
            here = ((dve_ln, dve_ln.count),)
            yield
            made[("xn", "x2n")[which], n] = here

        def norm1(n):
            need(dve, ld_x[n % 2])
            need(pool, ld_x[n % 2])
            need(pool, ld_w)
            for t in range(TT):
                pool_x2.did(pool.tensor_tensor(x2[:, n * TT + t], xin[n % 2][:, t], bo_b[:], ALU.add))
            yield from norm(n, 0, xin[n % 2], xn, ("xn", n - 1))

        def masks(n):
            need(act, ld_m[n % 2])
            need(act, dve_misc, weights_done)
            need(act, pe_s1, max(n - 2, 0) * H)
            for t in range(TT):
                act_bq.did(act.activation(Bq[n % 3][:, t], min_[n % 2][:, 0, t], ACT.Identity, bias=nbig[:],
                                          scale=padB[:, n * TT + t:n * TT + t + 1]))
            here = act_bq.count
            yield
            need(dve, ld_m[n % 2])
            need(dve, pe_s2, max(n - 2, 0) * H)
            dve_bk.did(dve.scalar_tensor_tensor(
                Bk[n % 3][:], min_[n % 2][:, 1], BIG, padR[:, n:n + 1].to_broadcast([P, TT, L]), ALU.mult, ALU.add))
            yield
            need(dve, act_bq, here)
            need(dve, dve_misc)
            dve_misc.did(dve.tensor_reduce(free_[:], Bq[n % 3][:], AX.X, ALU.max))
            need(dve, dve_misc)
            dve_misc.did(dve.tensor_scalar(free_[:], free_[:], 0.0, None, ALU.is_ge))
            yield
            need(dve, dve_misc)
            dve_misc.did(dve.reciprocal(free_[:], free_[:]))
            yield
            need(dve, dve_misc)
            dve_misc.did(dve.tensor_tensor(nanb[:, n * TT:(n + 1) * TT], free_[:], free_[:], ALU.subtract))

        def project(n, which, w, src):
            tag = (("x", "c")[which], n)
            while tag not in made:
                yield
            b = yield from claim()
            yield from wait_made(tag)
            for m in range(KC):
                i = product(bank[b][:, m * L:(m + 1) * L],
                            [lambda kc, m=m, q=q: w[q][:, kc, m * P:(m + 1) * P] for q in range(2)],
                            [lambda kc, q=q: src[q][:, kc, :] for q in range(2)])
            pe_misc.did(i)
            here = pe_misc.count
            yield
            need(act, pe_misc, here)
            need(dve, pe_misc, here)
            parts(bank[b][:].rearrange("p (k l) -> p k l", k=KC), flat[which][0][:], flat[which][1][:])
            give(b)
            here = ((act_misc, act_misc.count), (dve_misc, dve_misc.count))
            yield
            made[("q", "k")[which], n] = here

        def heads_rows(n, which, pick, m0, dst):
            tag = (("q", "k")[which], n)
            while tag not in made:
                yield
            b = yield from claim()
            yield from wait_made(tag)
            for m in range(m0, m0 + 2):
                chunk, s = divmod(2 * m, P // D)
                for part in range(2):
                    i = pe.matmul(bank[b][:, (m - m0) * L:(m - m0 + 1) * L], pick[part][:, s:s + 2].rearrange(
                        "p s c d -> p (s c d)"), flat[which][part][:, chunk, :], start=(part == 0), stop=(part == 1))
            pe_misc.did(i)
            here = pe_misc.count
            yield
            need(act, pe_misc, here)
            need(act, pe_s2, max(n - 2, 0) * H)
            act_misc.did(act.activation(dst[n % 3][:, m0:m0 + 2].rearrange("p m l -> p (m l)"), bank[b][:], ACT.Copy))
            give(b)
            ready[n] = ((act_misc, act_misc.count), (act_bq, act_bq.count))

        def values(n):
            b = yield from claim()
            for t in range(TT):
                i = product(bank[b][:, t * E:(t + 1) * E],
                            [lambda kc, t=t, q=q: cT[q][:, kc, t * P:(t + 1) * P] for q in range(2)],
                            [lambda kc, q=q: WvT[q][:, kc, :] for q in range(2)])
            pe_misc.did(i)
            here = pe_misc.count
            read["c", n] = here
            yield
            need(act, pe_misc, here)
            need(act, pool_c)
            need(act, pe_pv, max(n - 2, 0) * H)
            act_misc.did(act.activation(V[n % 3][:, :, :, 0:D],
                                        bank[b][:].rearrange("p (t h d) -> p t h d", t=TT, d=D), ACT.Copy))
            give(b)
            made["V", n] = ((act_misc, act_misc.count),)

        ready, maxima = {}, {}

        def max_rows(n):
            nm = nmax[n % 2][:].rearrange("p h (t o) -> p t o h", o=1).to_broadcast([P, TT, 2, H])
            hi, lo = mrep[:, :, :, 0, :], mrep[:, :, :, 1, :]
            need(dve, dve_max, (n + 1) * H)
            need(dve, pe_misc, read.get(("mrep", n - 1), 0))
            need(dve, pool_c)
            dve_misc.did(dve.tensor_copy(hi.bitcast(F32R), nm))
            need(dve, dve_misc)
            dve_misc.did(dve.tensor_tensor(lo.bitcast(F32R), nm, hi, ALU.subtract))
            written = dve_misc.count
            yield
            b = yield from claim()
            need(pe, dve_misc, written)
            for t in range(TT):
                i = pe.transpose(bank[b][:, t * P:(t + 1) * P], mrep[:, t].rearrange("p a c h -> p (a c h)"), ident[:])
            pe_misc.did(i)
            here = read["mrep", n] = pe_misc.count
            yield
            need(act, pe_misc, here)
            need(act, pe_s2, max(n - 1, 0) * H)
            act_misc.did(act.activation(mT[n % 2][:], bank[b][:, 0:L], ACT.Copy))
            give(b)
            maxima[n] = act_misc.count

        def head(g):
            n, h = divmod(g, H)
            return n, h, slice((h % 2) * HALF, (h % 2 + 1) * HALF), h // 2

        def scores_for_max(g):
            n, h, r, m = head(g)
            b = s1_bank[g % 2]
            for stage, count in ready[n]:
                need(pe, stage, count)
            need(pe, dve_max, max(g - 1, 0))
            pe.matmul(b[:], identb[:], Bq[n % 3][:].rearrange("p t l -> p (t l)"), start=True, stop=False,
                      unmasked=None)
            for t in range(TT):
                i = pe.matmul(b[:, t * L:(t + 1) * L], Q[n % 3][r, m, t * P:(t + 1) * P], K[n % 3][r, m, :],
                              start=False, stop=(t == TT - 1), unmasked=dict(start=True, stop=True))
            pe_s1.did(i)

        def take_max(g):
            n, h, _, _ = head(g)
            need(dve, pe_s1, g + 1)
            if h == 0:
                need(dve, dve_misc)
            dve_max.did(dve.tensor_reduce(nmax[n % 2][:, h, :], s1_bank[g % 2][:].rearrange("p (t k) -> p t k", t=TT),
                                          AX.X, ALU.max, negate=True))

        def scores(g):
            n, h, r, m = head(g)
            b = s2_bank[g % 2]
            need(pe, act_exp, max(g - 1, 0))
            need(pe, act_misc, maxima[n])
            need(pe, dve_bk, n + 1)
            pe.matmul(b[:], identb[:], Bk[n % 3][:].rearrange("p t l -> p (t l)"), start=True, stop=False,
                      unmasked=None)
            for t in range(TT):
                o = b[:, t * L:(t + 1) * L]
                pe.matmul(o, K[n % 3][r, m, t * P:(t + 1) * P], Q[n % 3][r, m, :], start=False, stop=False,
                          unmasked=dict(start=True))
                i = pe.matmul(o, sel[r, h, :], mT[n % 2][r, :], start=False, stop=(t == TT - 1),
                              unmasked=dict(stop=True))
            pe_s2.did(i)

        def exponentials(g):
            need(act, pe_s2, g + 1)
            need(act, pe_pv, max(g - 2, 0))
            act_exp.did(act.activation(prob[g % 3][:].rearrange("p t l -> p (t l)"), s2_bank[g % 2][:], ACT.Exp,
                                       scale=SCALE))

        def weighted(g):
            n, h, _, _ = head(g)
            j = h % OQ
            r = slice(j * OS, (j + 1) * OS)
            need(pe, act_exp, g + 1)
            for stage, count in made["V", n]:
                need(pe, stage, count)
            if j == 0:
                need(pe, dve_ot)
            for t in range(TT):
                i = pe.matmul(pv_bank[r, 0:L], V[n % 3][:, t, h, :], prob[g % 3][:, t, :], start=(t == 0),
                              stop=(t == TT - 1))
            pe_pv.did(i)

        def copy_out(g):
            n, h, _, _ = head(g)
            need(dve, pe_pv, g + 1)
            need(dve, pe_misc, read.get(("OT", n - 2), 0))
            dve_ot.did(dve.tensor_copy(OT[n % 2][h // OQ][:], pv_bank[:, 0:L]))

        def divide(n, t):
            yield
            b = yield from claim()
            need(pe, dve_ot, (n + 1) * H // OQ)
            for q in range(H // OQ):
                i = pe.transpose(bank[b][:, q * P:(q + 1) * P], OT[n % 2][q][:, t * P:(t + 1) * P], ident[:])
            pe_misc.did(i)
            here = pe_misc.count
            read["OT", n] = here
            yield
            need(dve, pe_misc, here)
            v = bank[b][:].rearrange("p (h c) -> p h c", c=OS)
            need(dve, dve_misc)
            dve_misc.did(dve.reciprocal(rden[:], v[:, :, D]))
            need(dve, dve_misc)
            dve_misc.did(dve.tensor_scalar(rden[:], rden[:], nanb[:, n * TT + t:n * TT + t + 1], None, ALU.add))
            need(dve, dve_misc)
            dve_misc.did(dve.tensor_tensor(ao[:, t].rearrange("p (h d) -> p h d", d=D), v[:, :, 0:D],
                                           rden[:].rearrange("p (h o) -> p h o", o=1).to_broadcast([P, H, D]),
                                           ALU.mult))
            give(b)
            here = ((dve_misc, dve_misc.count),)
            yield
            if t == TT - 1:
                made["ao", n] = here

        def output(n):
            while ("a", n) not in made:
                yield
            yield
            b = yield from claim()
            yield from wait_made(("a", n))
            for t in range(TT):
                i = product(bank[b][:, t * E:(t + 1) * E],
                            [lambda kc, t=t, q=q: aT[q][:, kc, t * P:(t + 1) * P] for q in range(2)],
                            [lambda kc, q=q: WoT[q][:, kc, :] for q in range(2)])
            pe_misc.did(i)
            here = pe_misc.count
            yield
            need(dve, pe_misc, here)
            need(dve, pool_x2)
            v = x2[:, n * TT:(n + 1) * TT]
            dve_misc.did(dve.tensor_tensor(v, bank[b][:].rearrange("p (t e) -> p t e", t=TT), v, ALU.add))
            give(b)
            yield
            need(dve, dve_misc)
            need(dve, st_list[n % 2])
            yield from norm(n, 1, v, x2n[n % 2], ("x2n", n - 2))

        def route(n):
            while ("y", n) not in made:
                yield
            b = yield from claim()
            yield from wait_made(("y", n))
            for t in range(TT):
                for kc in range(KC):
                    i = pe.matmul(bank[b][:, t * NE:(t + 1) * NE], yT[:, kc, t * P:(t + 1) * P], WgT[:, kc, :],
                                  start=(kc == 0), stop=(kc == KC - 1))
            pe_misc.did(i)
            here = pe_misc.count
            yield
            need(dve, pe_misc, here)
            raw = bank[b][:, 0:TT * NE].rearrange("p (t e) -> p t e", e=NE)
            dve_misc.did(dve.tensor_reduce(mx[:], raw, AX.X, ALU.max))

            def over(v):
                return v.rearrange("p (t o) -> p t o", o=1).to_broadcast([P, TT, NE])

            need(dve, dve_misc)
            need(dve, dve_gate)
            dve_misc.did(dve.tensor_tensor(lg[:], raw, over(mx[:]), ALU.subtract))
            give(b)
            yield
            need(act, dve_misc)
            act_gate.did(act.activation(lg[:], lg[:], ACT.Exp))
            yield
            need(dve, act_gate)
            dve_gate.did(dve.tensor_reduce(sm[:], lg[:], AX.X, ALU.add))
            need(dve, dve_gate)
            dve_gate.did(dve.reciprocal(sm[:], sm[:]))
            need(dve, dve_gate)
            dve_gate.did(dve.tensor_tensor(lg[:], lg[:], over(sm[:]), ALU.mult))
            yield
            need(dve, dve_gate)
            dve_gate.did(dve.tensor_scalar(gate[:], lg[:], 0.0, None, ALU.max))
            need(dve, dve_gate)
            shape = [P, TT, NE, NE]
            gj = gate[:].rearrange("p t (o e) -> p t o e", o=1).to_broadcast(shape)
            gi = gate[:].rearrange("p t (e o) -> p t e o", o=1).to_broadcast(shape)
            dve_gate.did(dve.tensor_tensor(larger[:], gj, gi, ALU.is_gt))
            dve_gate.did(dve.tensor_tensor(equal[:], gj, gi, ALU.is_equal))
            need(dve, dve_gate)
            dve_gate.did(dve.tensor_tensor(equal[:], equal[:], less[:].rearrange("p (o e) j -> p o e j", o=1)
                                           .to_broadcast(shape), ALU.mult))
            need(dve, dve_gate)
            dve_gate.did(dve.tensor_tensor(larger[:], larger[:], equal[:], ALU.add))
            need(dve, dve_gate)
            dve_gate.did(dve.tensor_reduce(rank[:], larger[:], AX.X, ALU.add))
            need(dve, dve_gate)
            T = slice(n * TT, (n + 1) * TT)
            dve_gate.did(dve.tensor_scalar(chosen[:, T], rank[:], float(TOP), None, ALU.is_lt))
            here = dve_gate.count
            yield
            yield
            yield
            b = yield from claim()
            need(pe, dve_gate, here)
            for t in range(TT):
                terms = [(before, chosen[:, n * TT + t])] + [(onesb, chosen[:, n * TT + u]) for u in range(t)]
                terms.append((onesb, run[:]))
                for k, (m, c) in enumerate(terms):
                    i = pe.matmul(bank[b][:, t * NE:(t + 1) * NE], m[:], c, start=(k == 0), stop=(k == len(terms) - 1))
            pe_misc.did(i)
            here = pe_misc.count
            need(dve, dve_gate)
            dve_gate.did(dve.tensor_tensor(weight[:, T], chosen[:, T], lg[:], ALU.mult))
            dve_gate.did(dve.tensor_copy(x2n[n % 2][:, :, E], ids[:, T]))
            dve_gate.did(dve.tensor_tensor(off[:], chosen[:, T], base[:].rearrange("p (o e) -> p o e", o=1)
                                           .to_broadcast([P, TT, NE]), ALU.mult))
            need(dve, dve_gate)
            dve_gate.did(dve.tensor_reduce(x2n[n % 2][:, :, E + 1], off[:], AX.X, ALU.add))
            yield
            need(dve, pe_misc, here)
            dve_misc.did(dve.tensor_tensor(place[:, T], bank[b][:, 0:TT * NE].rearrange("p (t e) -> p t e", e=NE),
                                           base[:].rearrange("p (o e) -> p o e", o=1).to_broadcast([P, TT, NE]),
                                           ALU.add))
            give(b)
            for t in range(TT):
                need(dve, dve_gate)
                dve_gate.did(dve.tensor_tensor(run[:], run[:], chosen[:, n * TT + t], ALU.add))
            yield
            need(dve, dve_misc)
            need(dve, dve_gate)
            dve_gate.did(dve.scalar_tensor_tensor(off[:], chosen[:, T], -FAR, place[:, T], ALU.mult, ALU.add))
            need(dve, dve_gate)
            dve_gate.did(dve.tensor_reduce(ends[:, 0], off[:], AX.X, ALU.min))
            need(dve, dve_gate)
            dve_gate.did(dve.tensor_tensor(off[:], chosen[:, T], place[:, T], ALU.mult))
            need(dve, dve_gate)
            dve_gate.did(dve.tensor_reduce(ends[:, 1], off[:], AX.X, ALU.max))
            need(dve, dve_gate)
            need(dve, st_list[n % 2])
            dve_gate.did(dve.tensor_scalar(rows[n % 2][:, 0], ends[:, 0], FAR, None, ALU.add))
            dve_gate.did(dve.tensor_copy(rows[n % 2][:, 1], ends[:, 1]))
            yield
            yield
            need(pool, dve_gate)
            need(pool, dve_ln)
            need(pool, st_zero)
            for t in range(TT):
                for k in range(TOP):
                    if t or k:
                        yield
                    st_list[n % 2].did(pool.indirect_dma_start(
                        out=lists, out_offset=bass.IndirectOffsetOnAxis(ap=rows[n % 2][:, k, t:t + 1], axis=0),
                        in_=x2n[n % 2][:, t], in_offset=None))

        LAG2, LAGV = 19, 20
        starts = {}

        def at(g, piece):
            starts.setdefault(g, []).append(piece)

        for n in range(NB):
            g0 = (n - 1) * H
            if n >= 2:
                at(g0 - 8, lambda n=n: iter([load(n)]))
            at(g0 - 2, lambda n=n: norm1(n))
            at(g0 + 0, lambda n=n: split_ctx(n))
            at(g0 + 1, lambda n=n: masks(n))
            at(g0 + 2, lambda n=n: project(n, 1, WkT, cT))
            for k, g in enumerate((2, 4, 6, 6)):
                at(g0 + g, lambda n=n, k=k: heads_rows(n, 1, pick_k, 2 * k, K))
            at(g0 + 3, lambda n=n: turn_rows(("xn", n), xn, ("x", n), xT))
            at(g0 + 5, lambda n=n: project(n, 0, WqT, xT))
            for k, g in enumerate((8, 8, 11, 13)):
                at(g0 + g, lambda n=n, k=k: heads_rows(n, 0, pick_q, 2 * k, Q))
            at(g0 + 15, lambda n=n: values(n))
            at((n + 1) * H, lambda n=n: max_rows(n))
            g1 = n * H + H - 1 + LAGV + 1
            at(g1 + 0, lambda n=n: divide(n, 0))
            at(g1 + 0, lambda n=n: divide(n, 1))
            at(g1 + 3, lambda n=n: turn_rows(("ao", n), ao, ("a", n), aT))
            at(g1 + 5, lambda n=n: output(n))
            at(g1 + 12, lambda n=n: turn_rows(("x2n", n), x2n[n % 2], ("y", n), [yT]))
            at(g1 + 13, lambda n=n: route(n))

        NG = NB * H
        going = []
        for g in range(min(starts), max(starts) + 2 * H):
            turns += given
            given.clear()
            if 0 <= g < NG:
                scores_for_max(g)
            if 0 <= g - LAG2 < NG:
                scores(g - LAG2)
            if 0 <= g - LAGV < NG:
                weighted(g - LAGV)
            if 0 <= g < NG:
                take_max(g)
            if 0 <= g - LAG2 < NG:
                exponentials(g - LAG2)
            if 0 <= g - LAGV < NG and (g - LAGV) % OQ == OQ - 1:
                copy_out(g - LAGV)
            going = [p for p in going if next(p, "end") != "end"]
            for piece in starts.get(g, []):
                p = piece()
                if next(p, "end") != "end":
                    going.append(p)
        assert not going

        with nc.tensor.If(hidden_keys):
            pe.write(masked=True)
        with nc.tensor.Else():
            pe.write(masked=False)
        pe = nc.tensor

        A.close()
        for engine in (sp, act, dve, pe, pool):
            for stage in (act_bq, dve_bk, dve_lo, pe_misc, dve_misc, act_misc, pe_pv, pe_s2, act_exp, dve_ln, dve_gate, dve_ot, pool_ln,
                          pool_x2):
                need(engine, stage)

        w1_in.append(sb(top, "w1_in1", [P, KC, F]))
        w2_in.append(sb(top, "w2_in1", [P, MF, E]))
        W1p = [[sb(top, f"W1p{i}{q}", [P, KC, F], F32R) for q in range(2)] for i in range(2)]
        W2p = [[sb(top, f"W2p{i}{q}", [P, MF, E], F32R) for q in range(2)] for i in range(2)]
        b2_in = [sb(top, f"b2_in{i}", [P, E]) for i in range(4)]
        b1c = [sb(top, f"b1c{i}", [P, MF]) for i in range(3)]
        xg = [sb(top, f"xg{i}", [P, TS // P, W]) for i in range(2)]
        slot = [sb(top, f"slot{i}", [P, TS // P], I32) for i in range(4)]
        xgT = [[sb(top, f"xgT{i}{q}", [P, KC, TS], F32R) for q in range(2)] for i in range(2)]
        hf = [sb(top, f"hf{i}", [P, 2, TS]) for i in range(2)]
        hp = [[sb(top, f"hp{i}{q}", [P, MF, TS], F32R) for q in range(2)] for i in range(2)]
        y = [sb(top, f"y{i}", [P, TS // P, E]) for i in range(2)]
        x_bank = [top.enter_context(nc.psum_tensor("x_bank", [P, 512], F32))]
        h_bank = [top.enter_context(nc.psum_tensor(f"h_bank{i}", [P, 2, TS], F32)) for i in range(4)]
        y_bank = [top.enter_context(nc.psum_tensor(f"y_bank{i}", [P, TS // P, E], F32)) for i in range(2)]
        n_bank = top.enter_context(nc.psum_tensor("n_bank", [P, NE], F32))

        count = sb(top, "count", [P, NE])
        steps = sb(top, "steps", [P, NE, MORE])
        extra = sb(top, "extra", [P, NE])
        prod = sb(top, "prod", [P, NE, NE])
        pre = sb(top, "pre", [P, NE])
        upto = sb(top, "upto", [P, NE])
        last = sb(top, "last", [P, 1])
        number = sb(top, "number", [P, EXTRA])
        over_ = sb(top, "over_", [P, EXTRA, NE])
        past = sb(top, "past", [P, EXTRA, NE])
        tile_e = sb(top, "tile_e", [P, EXTRA])
        tile_s = sb(top, "tile_s", [P, EXTRA])
        twice = sb(top, "twice", [P, EXTRA])
        table = sb(top, "table", [P, 2, EXTRA], I32)
        zrow = sb(top, "zrow", [P, NE], I32)
        beyond = sb(top, "beyond", [P, NT, NE])
        low = sb(top, "low", [P, NT])
        is_k = sb(top, "is_k", [P, 2, NT, NE])
        picked = sb(top, "picked", [P, NT, NE])
        gates = sb(top, "gates", [P, 2, NT])

        dve_r, pool_r, pe_r = step("dve_r"), step("pool_r"), step("pe_r")
        ld_xg = [step(f"ld_xg{i}", 16) for i in range(2)]
        ld_b2 = [step(f"ld_b2{i}", 16) for i in range(4)]
        act_w, dve_w1, dve_w2 = step("act_w"), step("dve_w1"), step("dve_w2")
        pe_xg, act_xg, dve_xg = step("pe_xg"), step("act_xg"), step("dve_xg")
        pe_h, act_h, dve_h = step("pe_h"), step("act_h"), step("dve_h")
        pe_y, dve_y = step("pe_y"), step("dve_y")
        dve_b1, act_b1, act_hi = step("dve_b1"), step("act_b1"), step("act_hi")
        st_y = [step(f"st_y{i}", 16) for i in range(4)]
        dve_slot = step("dve_slot")
        ld_r = [step(f"ld_r{i}", 16) for i in range(4)]
        dve_o = step("dve_o")
        st_out = step("st_out", 16)

        for k in range(MORE):
            pool_r.did(pool.memset(steps[:, :, k:k + 1], float(TS * (k + 1))))
        for k in range(EXTRA):
            pool_r.did(pool.memset(number[:, k:k + 1], float(k)))

        def tables():
            def row(v, shape):
                return v.rearrange("p (o e) -> p o e", o=1).to_broadcast(shape)

            def col(v, shape):
                return v.rearrange("p (e o) -> p e o", o=1).to_broadcast(shape)

            pe_r.did(pe.matmul(n_bank[:], onesb[:], run[:], start=True, stop=True))
            need(dve, pe_r)
            need(dve, pool_r)
            dve_r.did(dve.tensor_copy(count[:], n_bank[:]))
            yield
            need(dve, dve_r)
            dve_r.did(dve.tensor_tensor(zrow[:], count[:], base[:], ALU.add))
            yield
            need(dve, dve_r)
            dve_r.did(dve.tensor_tensor(steps[:], col(count[:], [P, NE, MORE]), steps[:], ALU.is_gt))
            yield
            need(dve, dve_r)
            dve_r.did(dve.tensor_reduce(extra[:], steps[:], AX.X, ALU.add))
            yield
            need(dve, dve_r)
            dve_r.did(dve.tensor_tensor(prod[:], row(extra[:], [P, NE, NE]), less[:], ALU.mult))
            yield
            need(dve, dve_r)
            dve_r.did(dve.tensor_reduce(pre[:], prod[:], AX.X, ALU.add))
            yield
            need(dve, dve_r)
            dve_r.did(dve.tensor_tensor(upto[:], pre[:], extra[:], ALU.add))
            yield
            need(dve, dve_r)
            dve_r.did(dve.tensor_scalar(last[:], upto[:, NE - 1:NE], -1.0, None, ALU.add))
            yield
            need(dve, dve_r)
            dve_r.did(dve.tensor_scalar(number[:], number[:], last[:], None, ALU.min))
            yield
            need(dve, dve_r)
            full = [P, EXTRA, NE]
            dve_r.did(dve.tensor_tensor(over_[:], row(upto[:], full), col(number[:], full), ALU.is_le))
            yield
            need(dve, dve_r)
            dve_r.did(dve.tensor_reduce(tile_e[:], over_[:], AX.X, ALU.add))
            yield
            need(dve, dve_r)
            dve_r.did(dve.tensor_tensor(past[:], over_[:], row(extra[:], full), ALU.mult))
            yield
            need(dve, dve_r)
            dve_r.did(dve.tensor_reduce(tile_s[:], past[:], AX.X, ALU.add))
            yield
            need(dve, dve_r)
            dve_r.did(dve.tensor_tensor(tile_s[:], number[:], tile_s[:], ALU.subtract))
            yield
            need(dve, dve_r)
            dve_r.did(dve.tensor_scalar(tile_s[:], tile_s[:], 1.0, float(TS), ALU.add, ALU.mult))
            yield
            need(dve, dve_r)
            dve_r.did(dve.scalar_tensor_tensor(table[:, 0], tile_e[:], float(REGION), tile_s[:], ALU.mult, ALU.add))
            yield
            need(dve, dve_r)
            dve_r.did(dve.tensor_copy(table[:, 1], tile_e[:]))
            yield
            need(dve, dve_r)
            dve_r.did(dve.tensor_scalar(twice[:], tile_e[:], 2.0 * REGION, None, ALU.mult))
            yield
            need(dve, dve_r)
            table_done.append(dve_r.count)

            wide = [P, NT, NE]
            dve_r.did(dve.scalar_tensor_tensor(beyond[:], chosen[:], -FAR, place[:], ALU.mult, ALU.add))
            yield
            need(dve, dve_r)
            dve_r.did(dve.tensor_reduce(low[:], beyond[:], AX.X, ALU.min))
            yield
            need(dve, dve_r)
            dve_r.did(dve.tensor_tensor(is_k[:, 0], beyond[:], col(low[:], wide), ALU.is_equal))
            yield
            need(dve, dve_r)
            dve_r.did(dve.tensor_tensor(is_k[:, 1], chosen[:], is_k[:, 0], ALU.subtract))
            yield
            need(dve, dve_r)
            for k in range(TOP):
                dve_r.did(dve.tensor_tensor(picked[:], is_k[:, k], weight[:], ALU.mult))
                yield
                need(dve, dve_r)
                dve_r.did(dve.tensor_reduce(gates[:, k], picked[:], AX.X, ALU.add))
                yield
                need(dve, dve_r)

        W1_d = W1.rearrange("e (k p) f -> e p k f", p=P)
        W2_d = W2.rearrange("e (m p) d -> e p m d", p=P)
        b2_d = b2.rearrange("(o e) d -> o e d", o=1)

        where = {}

        def load_weights(i):
            k = i % 2
            if i < NE:
                w1, w2, bb = W1_d[i], W2_d[i], b2_d[:, i, :]
            else:
                e = where[i][1]
                w1, w2 = (w[bass.ds(e, 1)].rearrange("o p a b -> (o p) a b") for w in (W1_d, W2_d))
                bb = b2_d[:, bass.ds(e, 1), :].rearrange("o u d -> o (u d)")
            if i > 1:
                need(sp, dve_w1, 2 * (i - 1))
            ld_w1[k].did(sp.dma_start(w1_in[k][:], w1))
            if i > 1:
                need(sp, dve_w2, 2 * (i - 1))
            ld_w2[k].did(sp.dma_start(w2_in[k][:], w2))
            need(sp, dve_y)
            ld_b2[i % 4].did(sp.dma_start(b2_in[i % 4][:], bb.to_broadcast([P, E])))

        def load_rows(i):
            k = i % 2
            if i >= NE:
                need(sp, dve_r, table_done[0])
                where[i] = (sp.value_load(table[0:1, 0, i - NE:i - NE + 1], min_val=0, max_val=NE * REGION - TS),
                            sp.value_load(table[0:1, 1, i - NE:i - NE + 1], min_val=0, max_val=NE - 1))
            if i == 0:
                need(sp, st_list[0])
                need(sp, st_list[1])
                need(sp, st_zero)
                ld_b2[0].did(sp.dma_start(b2_in[0][:], b2_d[:, 0, :].to_broadcast([P, E])))
            if i == NE:
                need(sp, ld_xg[0])
                need(sp, ld_xg[1])
                for e in range(NE):
                    z = sp.value_load(zrow[0:1, e:e + 1], min_val=e * REGION, max_val=e * REGION + REGION - TS)
                    st_zero.did(sp.dma_start(lists[bass.ds(z, TS), :].rearrange("(t p) e -> p t e", p=P), zero[:]))
                need(sp, st_zero)
            rows_ = lists[i * REGION:i * REGION + TS, :] if i < NE else lists[bass.ds(where[i][0], TS), :]
            need(sp, pe_xg)
            need(sp, dve_slot)
            ld_xg[k].did(sp.dma_start(xg[k][:], rows_.rearrange("(t p) e -> p t e", p=P)))

        def split(i, which, part):
            src, dst, ld, stage, reader = ((w1_in, W1p, ld_w1, dve_w1, pe_h), (w2_in, W2p, ld_w2, dve_w2, pe_y))[which]
            k = i % 2
            n = src[k].shape[1] // 2
            c = slice(part * n, (part + 1) * n)
            read_ = (MF // 2, 1)[which] * max(i - 1, 0)
            need(act, ld[k])
            need(act, reader, read_)
            act_w.did(act.activation(dst[k][0][:, c], src[k][:, c], ACT.Copy))
            yield
            need(dve, ld[k])
            need(dve, reader, read_)
            need(dve, act_w)
            stage.did(dve.tensor_tensor(dst[k][1][:, c], src[k][:, c], dst[k][0][:, c].bitcast(F32), ALU.subtract))

        def turn_tile(i):
            k = i % 2
            need(pe, ld_xg[k])
            need(pe, dve_xg)
            for kc in range(KC):
                for t in range(TS // P):
                    ins = pe.transpose(x_bank[0][:, kc * TS + t * P:kc * TS + (t + 1) * P],
                                       xg[k][:, t, kc * P:(kc + 1) * P], ident[:])
            pe_xg.did(ins)
            own = 2.0 * REGION * i if i < NE else twice[:, i - NE:i - NE + 1]
            need(dve, ld_xg[k])
            need(dve, st_y[i % 4])
            dve_slot.did(dve.scalar_tensor_tensor(slot[i % 4][:], xg[k][:, :, E + 1], own, xg[k][:, :, E],
                                                  ALU.is_lt, ALU.add))
            need(act, pe_xg)
            need(act, pe_h, max(i - 1, 0) * (MF // 2))
            v = x_bank[0][:].rearrange("p (k l) -> p k l", k=KC)
            act_xg.did(act.activation(xgT[k][0][:], v, ACT.Copy))
            need(dve, act_xg)
            dve_xg.did(dve.tensor_tensor(xgT[k][1][:], v, xgT[k][0][:].bitcast(F32), ALU.subtract))

        def bias1(i):
            if i < NE:
                return b1T[:, i * MF:(i + 1) * MF]
            e = dve.value_load(table[0:1, 1, i - NE:i - NE + 1], min_val=0, max_val=NE - 1)
            need(dve, act_h, (i - 2) * MF)
            need(dve, act_b1)
            dve_b1.did(dve.tensor_copy(b1c[i % 3][:], b1T[:, bass.ds(e * MF, MF)]))
            return b1c[i % 3][:]

        def hidden(i, pair):
            k = i % 2
            b = h_bank[pair]
            need(pe, act_h, max(act_h.count - 6, 0))
            if pair == 0:
                need(pe, dve_w1)
                need(pe, dve_xg)
            for u in range(2):
                m = 2 * pair + u
                terms = [(kc, a, c) for kc in range(KC) for a, c in ((0, 0), (0, 1), (1, 0))]
                for j, (kc, a, c) in enumerate(terms):
                    ins = pe.matmul(b[:, u, :], W1p[k][a][:, kc, m * P:(m + 1) * P], xgT[k][c][:, kc, :],
                                    start=(j == 0), stop=(j == len(terms) - 1))
            pe_h.did(ins)

        def gelu(i, pair, bias):
            need(act, pe_h, i * (MF // 2) + pair + 1)
            need(act, dve_h, max(dve_h.count - 1, 0))
            need(act, act_hi, max(act_hi.count - 1, 0))
            need(act, dve_b1, max(i - NE + 1, 0))
            for u in range(2):
                m = 2 * pair + u
                act_h.did(act.activation(hf[pair % 2][:, u], h_bank[pair][:, u], ACT.Gelu, bias=bias[:, m:m + 1]))

        def hidden_parts(i, pair):
            k = i % 2
            c = slice(2 * pair, 2 * pair + 2)
            need(act, act_h)
            need(act, pe_y)
            act_hi.did(act.activation(hp[k][0][:, c], hf[pair % 2][:], ACT.Copy))
            need(dve, act_hi)
            dve_h.did(dve.tensor_tensor(hp[k][1][:, c], hf[pair % 2][:], hp[k][0][:, c].bitcast(F32), ALU.subtract))

        def outputs(i, t):
            k = i % 2
            need(pe, dve_h, h_done[i])
            need(pe, dve_w2, 2 * (i + 1))
            need(pe, dve_y)
            terms = [(m, a, c) for m in range(MF) for a, c in ((0, 0), (0, 1), (1, 0))]
            for j, (m, a, c) in enumerate(terms):
                ins = pe.matmul(y_bank[k][:, t, :], hp[k][a][:, m, t * P:(t + 1) * P], W2p[k][c][:, m, :],
                                start=(j == 0), stop=(j == len(terms) - 1))
            if t == TS // P - 1:
                pe_y.did(ins)

        def store(i):
            k = i % 2
            need(dve, pe_y, i + 1)
            need(dve, ld_b2[i % 4])
            need(dve, st_y[(i - 2) % 4])
            for t in range(TS // P):
                dve_y.did(dve.tensor_tensor(y[k][:, t], y_bank[k][:, t], b2_in[i % 4][:], ALU.add))
            need(pool, dve_y)
            need(pool, dve_slot)
            for t in range(TS // P):
                for stage in st_y:
                    need(pool, stage)
                st_y[i % 4].did(pool.indirect_dma_start(
                    out=results, out_offset=bass.IndirectOffsetOnAxis(ap=slot[i % 4][:, t:t + 1], axis=0),
                    in_=y[k][:, t], in_offset=None))

        h_done = {}
        table_done = []
        load_weights(1)
        load_rows(0)
        load_rows(1)
        for j, which in ((0, 0), (0, 1), (1, 0)):
            for part in range(2):
                for _ in split(j, which, part):
                    pass
        need(act, pe_misc)
        act_b1.did(act.activation(b1c[0][:, 0:1], b1T[:, 0:1], ACT.Gelu))
        turn_tile(0)
        working = tables()
        next_bias = bias1(0)
        for i in range(NTILE + 1):
            if i < NTILE:
                bias, next_bias = next_bias, None
                for pair in range(MF // 2):
                    hidden(i, pair)
                    gelu(i, pair, bias)
                    which, j = (0, i + 1) if pair < 2 else (1, i)
                    s = split(j, which, pair % 2) if 0 < i and j < NTILE else iter(())
                    hidden_parts(i, pair)
                    next(s, None)
                    next(s, None)
                    for _ in range(2):
                        next(working, None)
                    if pair == 1 and i + 1 < NTILE:
                        turn_tile(i + 1)
                        next_bias = bias1(i + 1)
                    if pair == 2 and i + 2 < NTILE:
                        load_rows(i + 2)
                    if pair == 3 and i + 2 < NTILE:
                        load_weights(i + 2)
                h_done[i] = dve_h.count
            if i:
                for t in range(TS // P):
                    outputs(i - 1, t)
                store(i - 1)

        GT = 4
        got = [sb(top, f"got{i}", [P, GT, TOP, E]) for i in range(3)]
        r_d = results[1:1 + TOP * NT * P, :].rearrange("(t p k) e -> p t k e", p=P, k=TOP)
        need(dve, dve_r)
        for stage in st_y:
            need(sp, stage)

        def fetch(G):
            need(sp, dve_o)
            ld_r[G % 3].did(sp.dma_start(got[G % 3][:], r_d[:, G * GT:(G + 1) * GT]))

        for G in range(3):
            fetch(G)
        for G in range(NT // GT):
            need(dve, ld_r[G % 3])
            for k in range(TOP):
                for t in range(GT):
                    T = G * GT + t
                    need(dve, dve_o, max(dve_o.count - GT + 1, 0))
                    dve_o.did(dve.scalar_tensor_tensor(x2[:, T], got[G % 3][:, t, k], gates[:, k, T:T + 1], x2[:, T],
                                                       ALU.mult, ALU.add))
            if G + 3 < NT // GT:
                fetch(G + 3)
            need(act, dve_o)
            st_out.did(act.dma_start(out_d[:, G * GT:(G + 1) * GT], x2[:, G * GT:(G + 1) * GT]))
        need(sp, st_out)


def kernel(x, ctx_1024, mask_BxS2_bf1, mask_BxSxS2_bf1, L0_xattn_Wq, L0_xattn_Wk, L0_xattn_Wv, L0_xattn_Wo,
           L0_xattn_bo, L0_ffn_w_gate, L0_ffn_W1, L0_ffn_b1, L0_ffn_W2, L0_ffn_b2):
    import concourse.bacc as bacc
    from concourse.bass_utils import run_bass_kernel_spmd

    tokens, p = mask_BxS2_bf1.size, P
    named = dict(x=x, ctxT=ctx_1024.transpose(0, 2, 1), pad=mask_BxS2_bf1,
                 pad_c_in=mask_BxS2_bf1.reshape(tokens // p, p).T, mask=mask_BxSxS2_bf1,
                 maskT=mask_BxSxS2_bf1.transpose(0, 2, 1), WqT_in=L0_xattn_Wq.T, WkT_in=L0_xattn_Wk.T,
                 WvT_in=L0_xattn_Wv.T, WoT_in=L0_xattn_Wo.T, bo=L0_xattn_bo, wgT_in=L0_ffn_w_gate.T, W1=L0_ffn_W1,
                 b1T_in=L0_ffn_b1.reshape(-1, p).T, W2=L0_ffn_W2, b2=L0_ffn_b2)
    nc = bacc.Bacc("TRN2", target_bir_lowering=False, num_devices=1)
    arrays, args = {}, {}
    for name, a in named.items():
        a = np.ascontiguousarray(a)
        if a.dtype == bool:
            a = a.view(np.uint8)
        arrays[f"in_{name}"] = a
        args[name] = nc.dram_tensor(f"in_{name}", a.shape, mybir.dt.from_np(a.dtype), kind="ExternalInput").ap()
    out = nc.dram_tensor("out_0", np.shape(x), F32, kind="ExternalOutput").ap()
    build(nc, out=out, **args)
    r = run_bass_kernel_spmd(nc, [arrays], core_ids=[0])
    return r.results[0]["out_0"]
```
